# Optimizing a Trainium2 kernel written in Bass

```python
import numpy as np
import jax
import jax.numpy as jnp

def _softmax(x, axis=-1):
    return jax.nn.softmax(x, axis=axis)

def _gelu(x):
    return jax.nn.gelu(x, approximate=True)

def _silu(x):
    return jax.nn.silu(x)

def _sigmoid(x):
    return jax.nn.sigmoid(x)

def _layernorm(x, axis=-1, eps=1e-05):
    m = jnp.mean(x, axis=axis, keepdims=True)
    v = jnp.var(x, axis=axis, keepdims=True)
    return (x - m) / jnp.sqrt(v + eps)

def _scatter_add(tgt, idx, src, axis=0):
    return tgt.at[idx].add(src)

def _segment_sum(src, seg, n):
    return jax.ops.segment_sum(src, seg, n)
kernel_name = 'mk_adj_ffn_d2_adj_r2_9cb751'

def setup_inputs(seed: int=0):
    np.random.seed(seed)
    _w = jnp.asarray

    def _rec_inputs():
        import jax
        import jax.numpy as jnp
        _gk = jax.random.key(seed)
        x = -0.0005207 + 1.001 * jax.random.normal(jax.random.fold_in(_gk, 1), (4096, 128), jnp.float32)
        _a = jax.random.bernoulli(jax.random.fold_in(_gk, 2), 0.000488281, (4096, 4096))
        _a = jnp.logical_or(_a, jnp.swapaxes(_a, -1, -2))
        _a = jnp.logical_or(_a, jnp.eye(4096, dtype=bool))
        adj = _a.astype(jnp.int32)
        return (x, adj)
    x, adj = _rec_inputs()

    def _L0_gnn_setup():
        import jax, jax.numpy as jnp
        import numpy as np
        NEG_INF = -9000000000000000.0
        key = jax.random.key(seed)
        k1, k2, k3, k4 = jax.random.split(key, 4)
        N, F = (4096, 128)
        node = jax.random.normal(k1, (N, F), dtype=jnp.float32)
        adj = jax.random.randint(k2, (N, N), 0, 2, dtype=jnp.int32)
        W = jax.random.normal(k3, (F, F), dtype=jnp.float32) * (1.0 / np.sqrt(F))
        a = jax.random.normal(k4, (2 * F, 1), dtype=jnp.float32) * (1.0 / np.sqrt(F))
        return {'node': node, 'adj': adj, 'W': W, 'a': a}
    _L0_gnn_all = _L0_gnn_setup()
    _L0_gnn_in = {k: v for k, v in _L0_gnn_all.items() if k in ('W', 'a')}
    del _L0_gnn_all

    def _L0_ffn_setup():
        import jax, jax.numpy as jnp
        import numpy as np
        IN_CH = 128
        OUT_CH = 128
        key = jax.random.key(seed)
        kx, kw, kb = jax.random.split(key, 3)
        x = jax.random.normal(kx, (8, 2048, IN_CH), dtype=jnp.float32)
        bound = 1.0 / np.sqrt(IN_CH)
        weight = jax.random.uniform(kw, (OUT_CH, IN_CH), dtype=jnp.float32, minval=-bound, maxval=bound)
        bias = jax.random.uniform(kb, (OUT_CH,), dtype=jnp.float32, minval=-bound, maxval=bound)
        return {'x': x, 'weight': weight, 'bias': bias}
    _L0_ffn_all = _L0_ffn_setup()
    _L0_ffn_in = {k: v for k, v in _L0_ffn_all.items() if k in ('weight', 'bias')}
    del _L0_ffn_all

    def _L1_gnn_setup():
        import jax, jax.numpy as jnp
        import numpy as np
        ALPHA = 0.2
        key = jax.random.key(seed)
        k1, k2, k3, k4 = jax.random.split(key, 4)
        N, Fin, Fout = (4096, 128, 128)
        h = jax.random.normal(k1, (N, Fin), dtype=jnp.float32)
        adj = jax.random.randint(k2, (N, N), 0, 2, dtype=jnp.int32)
        wlim = np.sqrt(6.0 / (Fin + Fout)).astype(np.float32)
        W = jax.random.uniform(k3, (Fin, Fout), dtype=jnp.float32, minval=-wlim, maxval=wlim)
        alim = np.sqrt(6.0 / (2 * Fout + 1)).astype(np.float32)
        a = jax.random.uniform(k4, (2 * Fout, 1), dtype=jnp.float32, minval=-alim, maxval=alim)
        return {'h': h, 'adj': adj, 'W': W, 'a': a}
    _L1_gnn_all = _L1_gnn_setup()
    _L1_gnn_in = {k: v for k, v in _L1_gnn_all.items() if k in ('W', 'a')}
    del _L1_gnn_all

    def _L1_ffn_setup():
        import jax, jax.numpy as jnp
        import numpy as np
        D_MODEL = 128
        EXPERT_DIM = 256
        NUM_EXPERTS = 8
        TOP_K = 2
        SEQ_LEN = 1024
        BATCH = 2
        key = jax.random.key(seed)
        ks = jax.random.split(key, 8)
        s = 0.02
        x = jax.random.normal(ks[0], (SEQ_LEN, BATCH, D_MODEL), dtype=jnp.float32)
        Wg = jax.random.normal(ks[1], (D_MODEL, NUM_EXPERTS), dtype=jnp.float32) * s
        bg = jax.random.normal(ks[2], (NUM_EXPERTS,), dtype=jnp.float32) * s
        bias = jnp.zeros((NUM_EXPERTS,), dtype=jnp.float32)
        W1 = jax.random.normal(ks[3], (NUM_EXPERTS, D_MODEL, EXPERT_DIM), dtype=jnp.float32) * s
        b1 = jax.random.normal(ks[4], (NUM_EXPERTS, EXPERT_DIM), dtype=jnp.float32) * s
        W2 = jax.random.normal(ks[5], (NUM_EXPERTS, EXPERT_DIM, D_MODEL), dtype=jnp.float32) * s
        b2 = jax.random.normal(ks[6], (NUM_EXPERTS, D_MODEL), dtype=jnp.float32) * s
        return {'x': x, 'Wg': Wg, 'bg': bg, 'bias': bias, 'W1': W1, 'b1': b1, 'W2': W2, 'b2': b2}
    _L1_ffn_all = _L1_ffn_setup()
    _L1_ffn_in = {k: v for k, v in _L1_ffn_all.items() if k in ('Wg', 'bg', 'bias', 'W1', 'b1', 'W2', 'b2')}
    del _L1_ffn_all
    return {'x': x, 'adj': adj, 'L0_gnn_W': _L0_gnn_in['W'], 'L0_gnn_a': _L0_gnn_in['a'], 'L0_ffn_weight': _L0_ffn_in['weight'], 'L0_ffn_bias': _L0_ffn_in['bias'], 'L1_gnn_W': _L1_gnn_in['W'], 'L1_gnn_a': _L1_gnn_in['a'], 'L1_ffn_Wg': _L1_ffn_in['Wg'], 'L1_ffn_bg': _L1_ffn_in['bg'], 'L1_ffn_bias': _L1_ffn_in['bias'], 'L1_ffn_W1': _L1_ffn_in['W1'], 'L1_ffn_b1': _L1_ffn_in['b1'], 'L1_ffn_W2': _L1_ffn_in['W2'], 'L1_ffn_b2': _L1_ffn_in['b2']}

def reference(x, adj, L0_gnn_W, L0_gnn_a, L0_ffn_weight, L0_ffn_bias, L1_gnn_W, L1_gnn_a, L1_ffn_Wg, L1_ffn_bg, L1_ffn_bias, L1_ffn_W1, L1_ffn_b1, L1_ffn_W2, L1_ffn_b2):
    import jax
    import jax.numpy as jnp

    def _L0_gnn_ref(node, adj, W, a):
        import jax, jax.numpy as jnp
        import numpy as np
        NEG_INF = -9000000000000000.0
        h = node @ W
        Fdim = W.shape[0]
        s1 = h @ a[:Fdim, 0]
        s2 = h @ a[Fdim:, 0]
        e = jax.nn.leaky_relu(s1[:, None] + s2[None, :], negative_slope=0.01)
        e = jnp.where(adj > 0, e, jnp.float32(NEG_INF))
        att = jax.nn.softmax(e, axis=1)
        return h + att @ node

    def _L0_ffn_ref(x, weight, bias):
        import jax, jax.numpy as jnp
        import numpy as np
        IN_CH = 128
        OUT_CH = 128
        return jnp.einsum('bsi,oi->bso', x, weight) + bias

    def _L1_gnn_ref(h, adj, W, a):
        import jax, jax.numpy as jnp
        import numpy as np
        ALPHA = 0.2
        Fout = W.shape[1]
        Wh = h @ W
        a1, a2 = (a[:Fout, 0], a[Fout:, 0])
        f1 = Wh @ a1
        f2 = Wh @ a2
        e = jax.nn.leaky_relu(f1[:, None] + f2[None, :], negative_slope=ALPHA)
        e = jnp.where(adj == 0, -jnp.inf, e)
        attention = jax.nn.softmax(e, axis=1)
        h_prime = attention @ Wh
        return h_prime

    def _L1_ffn_ref(x, Wg, bg, bias, W1, b1, W2, b2):
        import jax, jax.numpy as jnp
        import numpy as np
        D_MODEL = 128
        EXPERT_DIM = 256
        NUM_EXPERTS = 8
        TOP_K = 2
        SEQ_LEN = 1024
        BATCH = 2
        x_flat = x.reshape(-1, D_MODEL)
        gate_logits = x_flat @ Wg + bg + bias
        topk_vals, topk_idx = jax.lax.top_k(gate_logits, TOP_K)
        topk_w = jax.nn.softmax(topk_vals, axis=-1)
        combine = (jax.nn.one_hot(topk_idx, NUM_EXPERTS, dtype=x.dtype) * topk_w[..., None]).sum(axis=1)
        h = jax.nn.relu(jnp.einsum('td,edh->teh', x_flat, W1) + b1)
        y = jnp.einsum('teh,ehd->ted', h, W2) + b2
        out = jnp.einsum('ted,te->td', y, combine)
        return out.reshape(x.shape)
    x = x + _L0_gnn_ref(_layernorm(x, axis=-1), adj, L0_gnn_W, L0_gnn_a)
    x = x + _L0_ffn_ref(_layernorm(x, axis=-1)[None], L0_ffn_weight, L0_ffn_bias)[0]
    x = x + _L1_gnn_ref(_layernorm(x, axis=-1), adj, L1_gnn_W, L1_gnn_a)
    x = x + _L1_ffn_ref(_layernorm(x, axis=-1)[None], L1_ffn_Wg, L1_ffn_bg, L1_ffn_bias, L1_ffn_W1, L1_ffn_b1, L1_ffn_W2, L1_ffn_b2)[0]
    return x

_drawn_inputs = setup_inputs


def setup_inputs(seed=0):
    import zlib

    import numpy as np

    out = dict(_drawn_inputs(seed))
    spreads = {'L1_ffn_bias': (0.0, 0.795)}
    factors = {'L1_ffn_Wg': 3.274,
     'L1_ffn_bg': 8.0,
     'L1_ffn_W1': 3.767,
     'L1_ffn_b1': 8.0,
     'L1_ffn_W2': 3.124,
     'L1_ffn_b2': 7.807}
    for name, (base, spread) in spreads.items():
        noise = np.random.default_rng([zlib.crc32(name.encode()), seed]).standard_normal(out[name].shape)
        drawn = base * np.exp(spread * noise) if base else spread * noise
        out[name] = jnp.asarray(drawn.astype(out[name].dtype))
    for name, factor in factors.items():
        out[name] = (out[name] * factor).astype(out[name].dtype)
    return out
```

```python
from contextlib import ExitStack

import numpy as np

import concourse.bass as bass
from concourse import mybir

F32 = mybir.dt.float32
F16 = mybir.dt.float16
F8 = mybir.dt.float8e4
U8 = mybir.dt.uint8
U32 = mybir.dt.uint32
ALU = mybir.AluOpType
ACT = mybir.ActivationFunctionType
AX = mybir.AxisListType

N = 4096
P = 128
F = 128
TILES = N // P
GROUPS = 4
SUB = 4
PANELS = TILES // SUB
PW = SUB * P
E = 8
HID = 256
HB = HID // P
EPS = 1e-5
ALPHAS = (0.01, 0.2)
ONE_BIT = 5
ONE = float(1 << ONE_BIT)
VCOLS = 2 * (F + 1)
V_SCALE = 256.0
LOW = 2048.0


def gnn_moe_kernel(nc, x, adj, W0, a0, Wf, bf, W1, a1, Wg, bg, gbias, We1, be1, We2, be2, out):
    x_g = x.rearrange("(g c q s) f -> g q c (s f)", g=GROUPS, c=PANELS, q=32, s=SUB)
    out_g = out.rearrange("(g c q s) f -> g q c (s f)", g=GROUPS, c=PANELS, q=32, s=SUB)
    adj_g = adj.rearrange("(b c q s) (g k) -> c s g q b k", b=GROUPS, c=PANELS, q=32, s=SUB, g=GROUPS)

    with ExitStack() as ctx:
        def sb(name, shape, dt):
            return ctx.enter_context(nc.sbuf_tensor(name, shape, dt))

        def wait_alone(eng, semaphore, value):
            eng.wait_ge(semaphore, value)
            eng.sem_inc(passed[str(eng.engine)], 1)

        def sem(name):
            return ctx.enter_context(nc.semaphore(name))

        passed = {str(e.engine): sem(f"passed_{n}") for n, e in (("pe", nc.tensor), ("dve", nc.vector))}
        s1_rows = nc.dram_tensor("s1_rows", [2, TILES, P], F32)

        mask = sb("mask", [P, PANELS, PANELS, PW * SUB], U8)
        X = sb("X", [P, TILES, F], F32)
        V = [sb(f"V{m}", [P, TILES, VCOLS], F16) for m in range(2)]
        s1_row = sb("s1_row", [P, 2, PW], F32)
        ident = sb("ident", [P, P], F32)
        S12 = sb("S12", [P, 2, TILES], F32)
        neg_s2 = sb("neg_s2", [P, TILES], F32)
        AC = sb("AC", [P, 2, TILES], F32)
        AC_low = sb("AC_low", [P, 2, TILES], F32)
        eps_t = sb("eps_t", [P, 1], F32)
        smax = sb("smax", [P, 2], F32)
        stats = sb("stats", [P, SUB, 6], F32)
        mv = sb("mv", [P, SUB, 2], F32)
        rr = sb("rr", [P, 4, SUB], F32)
        BD = sb("BD", [P, 2, TILES], F32)
        den = sb("den", [P, 2, TILES], F32)
        warg = sb("warg", [P, 3, TILES], F32)
        scratch = sb("scratch", [P, 22544], U8)

        def at(buf, start, shape, dt, size):
            n = int(np.prod(shape))
            flat = buf[:, start:start + n * size].bitcast(dt)
            if len(shape) == 1:
                return flat
            names = "abcd"[:len(shape)]
            return flat.rearrange(f"p ({' '.join(names)}) -> p {' '.join(names)}",
                                  **{k: v for k, v in zip(names, shape)})

        raw = [at(scratch, 4096 * n, [GROUPS, 1024], U8, 1) for n in range(2)]
        turned = at(scratch, 8192, [PANELS, P], U32, 4)
        gate8 = at(scratch, 8192, [PW, SUB], U8, 1)
        ring = [[at(scratch, 12288 + 4096 * n + 2048 * m, [PW * SUB], U8, 1) for m in range(2)] for n in range(2)]
        scaled = at(scratch, 20480, [2, VCOLS], F32, 4)
        summed = sb("summed", [P, SUB, F + 1], F32)
        rden = sb("rden", [P, SUB], F32)
        mask_flat = mask[:].rearrange("p a b c -> p (a b c)")
        late = mask_flat[:, 5 * 16384:]

        def stage_buffers(buf):
            o = [0]

            def take(shape, dt=F32, size=4):
                r = at(buf, o[0], shape, dt, size)
                o[0] += int(np.prod(shape)) * size
                return r
            return take

        PS = ctx.enter_context(nc.psum_tensor("PS", [P, 8, 512], F32))

        def acc(ib, m):
            return PS[:, 2 * ib + m, 0:VCOLS]

        raw_ready = [sem(f"raw_ready{n}") for n in range(2)]

        def load_adj(pool, w, s):
            for g in range(GROUPS):
                pool.dma_start(raw[s % 2][32 * g:32 * g + 32], adj_g[w, s, g], max_dma_last_dim=4096)\
                    .then_inc(raw_ready[s % 2], 16)

        def node_stage(layer):
            L = f"n{layer}_"
            take = stage_buffers(late if layer == 0 else scratch)
            val = take([TILES, F])
            normed = s1_row[:, 0, :].rearrange("p (s f) -> p s f", s=SUB)
            normed_T = s1_row[:, 1, :]
            W_ext = take([F + 2])
            Wf_T = take([F])
            bias_row = take([F])
            tmp = take([SUB, F])
            W_T = tmp[:, 0, :]
            Wf_in = tmp[:, 1, :]
            a_cols = tmp[:, 2, 0:2]
            s1_T = at(scratch, 12288, [P], F32, 4) if layer == 0 else normed_T[:, 0:P]
            W, a, alpha = ((W0, a0, ALPHAS[0]), (W1, a1, ALPHAS[1]))[layer]

            loaded = sem(L + "loaded")
            ident_ready = sem(L + "ident_ready")
            weights_T = sem(L + "weights_T")
            weights_in = sem(L + "weights_in")
            wa_done = sem(L + "wa_done")
            wa_in = sem(L + "wa_in")
            chain = sem(L + "chain")
            var_ready = sem(L + "var_ready")
            root_ready = sem(L + "root_ready")
            normed_ready = sem(L + "normed_ready")
            turned_done = sem(L + "turned_done")
            turned_in = sem(L + "turned_in")
            prod_done = sem(L + "prod_done")
            prod_used = sem(L + "prod_used")
            s12_in = sem(L + "s12_in")
            val_in = sem(L + "val_in")
            pmax = sem(L + "pmax")
            allmax = sem(L + "allmax")
            args_ready = sem(L + "args_ready")
            exps_ready = sem(L + "exps_ready")
            s1T_done = sem(L + "s1T_done")
            s1T_in = sem(L + "s1T_in")
            rows_out = sem(L + "rows_out")
            v_full = sem(L + "v_full")
            v_high = sem(L + "v_high")
            v_rest = sem(L + "v_rest")
            v_low = sem(L + "v_low")
            fin = sem(L + "fin")

            passes = 2 if layer else 1
            n_loads = (4 + 2) if layer == 0 else 4
            block = ctx2.enter_context(nc.Block())

            @block.sync
            def _(sp):
                if layer == 0:
                    for g in range(GROUPS):
                        sp.dma_start(X[32 * g:32 * g + 32].rearrange("p (c s) f -> p c (s f)", s=SUB), x_g[g])\
                            .then_inc(loaded, 16)
                sp.dma_start(W_ext[:, 0:F], W).then_inc(loaded, 16)
                with nc.allow_non_contiguous_dma(reason="256 scalars"):
                    sp.dma_start(a_cols, a.rearrange("(c p) one -> p (c one)", c=2)).then_inc(loaded, 16)
                if layer == 1:
                    sp.dma_start(Wf_in, Wf).then_inc(loaded, 16)
                    sp.dma_start(bias_row, bf.rearrange("(o f) -> o f", o=1).to_broadcast((P, F)))\
                        .then_inc(loaded, 16)
                sp.wait_ge(s1T_in, 1)
                sp.dma_start(s1_rows[layer], s1_T[0:TILES, :]).then_inc(rows_out, 16)
                sp.wait_ge(rows_out, 16)

            @block.gpsimd
            def _(pool):
                if layer == 0:
                    nc.gpsimd.memset(ident[:], 0.0).then_inc(ident_ready, 1)
                    nc.gpsimd.memset(eps_t[:], EPS).then_inc(ident_ready, 1)
                    pool.wait_ge(ident_ready, 2)
                    nc.gpsimd.affine_select(out=ident[:], in_=ident[:], compare_op=ALU.not_equal, fill=1.0,
                                            base=0, pattern=[[-1, P]], channel_multiplier=1).then_inc(ident_ready, 1)
                    for s in range(2):
                        load_adj(pool, 0, s)
                pool.wait_ge(pmax, 1)
                nc.gpsimd.partition_all_reduce(smax[:, 1:2], smax[:, 0:1], P, bass.bass_isa.ReduceOp.max)\
                    .then_inc(allmax, 1)

            @block.tensor
            def _(pe):
                if layer == 0:
                    pe.wait_ge(ident_ready, 3)
                pe.wait_ge(loaded, 16 * n_loads)
                last = nc.tensor.transpose(PS[:, 0, 0:P], W_ext[:, 0:F], ident[:])
                if layer == 1:
                    last = nc.tensor.transpose(PS[:, 0, P:2 * P], Wf_in, ident[:])
                last.then_inc(weights_T, 1)
                pe.wait_ge(weights_in, 1)
                nc.tensor.matmul(PS[:, 1, 0:2], W_T, a_cols, start=True, stop=True).then_inc(wa_done, 1)
                pe.wait_ge(wa_in, 1)
                with pe.Fori(0, PANELS) as c:
                    for k in range(passes):
                        pe.wait_ge(normed_ready, passes * c + k + 1)
                        for s in range(SUB):
                            last = nc.tensor.transpose(PS[:, 0, s * P:s * P + P], normed[:, s, :], ident[:])
                        last.then_inc(turned_done, 1)
                        pe.wait_ge(turned_in, passes * c + k + 1)
                        pe.wait_ge(prod_used, passes * c + k + 1)
                        rhs = Wf_T if k < passes - 1 else W_ext
                        for s in range(SUB):
                            o = PS[:, 1 + s // 2, 256 * (s % 2):256 * (s % 2) + rhs.shape[1]]
                            last = nc.tensor.matmul(o, normed_T[:, s * P:s * P + P], rhs, start=True, stop=True)
                        last.then_inc(prod_done, 1)
                pe.wait_ge(s12_in, PANELS)
                nc.tensor.transpose(PS[0:TILES, 0, 0:P], S12[:, 0, :], ident[:]).then_inc(s1T_done, 1)

            products = PS[:, 1:3, :].rearrange("p b (h f) -> p (b h) f", h=2)

            @block.scalar
            def _(act):
                act.wait_ge(weights_T, 1)
                if layer == 1:
                    nc.scalar.copy(Wf_T, PS[:, 0, P:2 * P])
                nc.scalar.copy(W_T, PS[:, 0, 0:P]).then_inc(weights_in, 1)
                act.wait_ge(wa_done, 1)
                nc.scalar.copy(W_ext[:, F:F + 2], PS[:, 1, 0:2]).then_inc(wa_in, 1)
                with act.Fori(0, PANELS) as c:
                    for k in range(passes):
                        act.wait_ge(var_ready, passes * c + k + 1)
                        nc.scalar.activation(rr[:, 1, :], rr[:, 0, :], ACT.Sqrt).then_inc(root_ready, 1)
                        act.wait_ge(turned_done, passes * c + k + 1)
                        nc.scalar.copy(normed_T, PS[:, 0, :]).then_inc(turned_in, 1)
                        if layer == 0:
                            nc.scalar.copy(val[:, bass.ds(c * SUB, SUB), :], normed[:]).then_inc(val_in, 1)
                    act.wait_ge(prod_done, passes * c + passes)
                    if layer == 1:
                        nc.scalar.copy(val[:, bass.ds(c * SUB, SUB), :], products[:, :, 0:F]).then_inc(val_in, 1)
                    nc.scalar.copy(S12[:, :, bass.ds(c * SUB, SUB)].rearrange("p k s -> p s k"),
                                   products[:, :, F:F + 2]).then_inc(s12_in, 1)
                act.wait_ge(s1T_done, 1)
                nc.scalar.copy(s1_T[0:TILES, :], PS[0:TILES, 0, 0:P]).then_inc(s1T_in, 1)
                act.wait_ge(args_ready, 1)
                nc.scalar.activation(AC[:], warg[:, 0:2, :], ACT.Exp).then_inc(exps_ready, 1)
                nc.scalar.activation(BD[:, 0, :], warg[:, 2, :], ACT.Exp).then_inc(exps_ready, 1)
                nc.scalar.activation(BD[:, 1, :], warg[:, 2, :], ACT.Exp, scale=alpha).then_inc(exps_ready, 1)
                act.wait_ge(v_full, 1)
                for m in range(2):
                    last = nc.scalar.copy(V[m][:, :, F], den[:, m, :])
                last.then_inc(v_high, 1)
                act.wait_ge(v_rest, 1)
                for m in range(2):
                    last = nc.scalar.mul(V[m][:, :, 2 * F + 1], den[:, m, :], LOW)
                last.then_inc(v_low, 1)
                with act.Fori(0, PANELS) as c:
                    for m in range(2):
                        tiles = V[m][:, bass.ds(c * SUB, SUB), :]
                        act.wait_ge(v_full, 2 * c + m + 2)
                        nc.scalar.copy(tiles[:, :, 0:F], tmp[:]).then_inc(v_high, 1)
                        act.wait_ge(v_rest, 2 * c + m + 2)
                        nc.scalar.mul(tiles[:, :, F + 1:2 * F + 1], tmp[:], LOW).then_inc(v_low, 1)

            @block.vector
            def _(dve):
                chained = [0]
                per = [0]

                def link(ins, base=0):
                    chained[0] += 1
                    ins.then_inc(chain, 1)
                    wait_alone(dve, chain, base + chained[0])

                dve.sem_inc(prod_used, 1)
                dve.wait_ge(loaded, 16 * n_loads)
                if layer == 0:
                    dve.wait_ge(ident_ready, 3)
                links = 6 * passes + (passes - 1)
                with dve.Fori(0, PANELS) as c:
                    base = c * links
                    for k in range(passes):
                        for s in range(SUB):
                            last = nc.vector.bn_stats(stats[:, s, :], X[:, c * SUB + s, :])
                        link(last, base)
                        for s in range(SUB):
                            last = nc.vector.bn_aggr(mv[:, s, :], stats[:, s, :])
                        link(last, base)
                        nc.vector.tensor_scalar(rr[:, 0, :], mv[:, :, 1], EPS, None, ALU.add).then_inc(var_ready, 1)
                        dve.wait_ge(root_ready, passes * c + k + 1)
                        link(nc.vector.reciprocal(rr[:, 2, :], rr[:, 1, :]), base)
                        link(nc.vector.tensor_tensor(rr[:, 3, :], rr[:, 2, :], rr[:, 2, :], ALU.mult), base)
                        link(nc.vector.tensor_tensor(rr[:, 3, :], rr[:, 3, :], rr[:, 0, :], ALU.mult), base)
                        link(nc.vector.tensor_scalar(rr[:, 3, :], rr[:, 3, :], -0.5, 1.5, ALU.mult, ALU.add), base)
                        nc.vector.tensor_tensor(rr[:, 2, :], rr[:, 2, :], rr[:, 3, :], ALU.mult)\
                            .then_inc(fin, 1)
                        dve.wait_ge(fin, passes * c + k + 1)
                        if k:
                            dve.wait_ge(turned_done, passes * c + k)
                        for s in range(SUB):
                            last = nc.vector.tensor_scalar(normed[:, s, :], X[:, c * SUB + s, :], mv[:, s, 0:1],
                                                           rr[:, 2, s:s + 1], ALU.subtract, ALU.mult)
                        last.then_inc(normed_ready, 1)
                        dve.wait_ge(prod_done, passes * c + k + 1)
                        x4 = X[:, bass.ds(c * SUB, SUB), :]
                        if k < passes - 1:
                            last = nc.vector.tensor_tensor(x4, x4, products[:, :, 0:F], ALU.add)
                            last.then_inc(prod_used, 1)
                            dve.wait_ge(prod_used, passes * c + k + 2)
                            link(nc.vector.tensor_tensor(x4, x4,
                                                         bias_row.rearrange("p (o f) -> p o f", o=1)
                                                         .to_broadcast((P, SUB, F)), ALU.add), base)
                        elif layer == 0:
                            dve.wait_ge(s12_in, c + 1)
                            dve.wait_ge(val_in, c + 1)
                            nc.vector.tensor_tensor(x4, x4, products[:, :, 0:F], ALU.add).then_inc(prod_used, 1)
                        else:
                            dve.wait_ge(s12_in, c + 1)
                            dve.wait_ge(val_in, c + 1)
                            dve.sem_inc(prod_used, 1)
                assert chained[0] == links, chained[0]
                chained[0] = links * PANELS
                nc.vector.tensor_reduce(smax[:, 0:1], S12[:, 1, :], AX.X, ALU.max).then_inc(pmax, 1)
                nc.vector.tensor_scalar(neg_s2[:], S12[:, 1, :], -1.0, None, ALU.mult)
                dve.wait_ge(allmax, 1)
                nc.vector.tensor_scalar(warg[:, 2, :], S12[:, 1, :], smax[:, 1:2], None, ALU.subtract)
                link(nc.vector.tensor_scalar(warg[:, 0, :], S12[:, 0, :], smax[:, 1:2], 1.0 - alpha,
                                             ALU.add, ALU.mult))
                link(nc.vector.tensor_scalar(warg[:, 1, :], warg[:, 0, :], -1.0, 0.0, ALU.mult, ALU.min))
                nc.vector.tensor_scalar(warg[:, 0, :], warg[:, 0, :], 0.0, None, ALU.min).then_inc(args_ready, 1)
                dve.wait_ge(exps_ready, 3)
                nc.vector.tensor_scalar(AC_low[:], AC[:], 1.0 / LOW, None, ALU.mult)
                link(nc.vector.tensor_scalar(BD[:], BD[:], V_SCALE, None, ALU.mult))
                nc.vector.tensor_copy(den[:], BD[:]).then_inc(v_full, 1)
                dve.wait_ge(v_high, 1)
                for m in range(2):
                    last = nc.vector.tensor_tensor(den[:, m, :], den[:, m, :], V[m][:, :, F], ALU.subtract)
                last.then_inc(v_rest, 1)
                with dve.Fori(0, PANELS) as c:
                    for m in range(2):
                        tiles = V[m][:, bass.ds(c * SUB, SUB), :]
                        factor = BD[:, m, bass.ds(c * SUB, SUB)].rearrange("p (s o) -> p s o", o=1)\
                            .to_broadcast((P, SUB, F))
                        dve.wait_ge(v_low, 2 * c + m + 1)
                        nc.vector.tensor_tensor(tmp[:], val[:, bass.ds(c * SUB, SUB), :], factor, ALU.mult)\
                            .then_inc(v_full, 1)
                        dve.wait_ge(v_high, 2 * c + m + 2)
                        nc.vector.tensor_tensor(tmp[:], tmp[:], tiles[:, :, 0:F], ALU.subtract).then_inc(v_rest, 1)
                dve.wait_ge(v_low, 2 * PANELS + 1)

        def attention_stage(layer):
            L = f"a{layer}_"
            row_loaded = sem(L + "row_loaded")
            turned_ready = sem(L + "turned_ready")
            raw_used = sem(L + "raw_used")
            mask_ready = sem(L + "mask_ready")
            gates = sem(L + "gates")
            m1_ready = sem(L + "m1_ready")
            masks_ready = sem(L + "masks_ready")
            masks_used = sem(L + "masks_used")
            acc_done = sem(L + "acc_done")
            acc_scaled = sem(L + "acc_scaled")
            scaled_used = sem(L + "scaled_used")
            added = sem(L + "added")
            summed_ready = sem(L + "summed_ready")
            rden_ready = sem(L + "rden_ready")
            summed_used = sem(L + "summed_used")
            block = ctx2.enter_context(nc.Block())

            def row(w):
                return s1_rows[layer, bass.ds(w * SUB, SUB), :].rearrange("(o s) p -> o (s p)", o=1)\
                    .to_broadcast((P, PW))

            @block.sync
            def _(sp):
                sp.dma_start(s1_row[:, 0, :], row(0)).then_inc(row_loaded, 16)
                sp.wait_ge(row_loaded, 16)
                sp.dma_start(s1_row[:, 1, :], row(1)).then_inc(row_loaded, 16)
                with sp.Fori(2, PANELS) as w:
                    sp.wait_ge(row_loaded, 16 * w)
                    sp.wait_ge(gates, PANELS * (w - 1))
                    sp.dma_start(s1_row[:, w % 2, :], row(w)).then_inc(row_loaded, 16)

            def turn(dve, w, n):
                if not (isinstance(w, int) and 4 * w + n == 0):
                    dve.wait_ge(mask_ready, 4 * w + n)
                dve.wait_ge(raw_ready[n % 2], 64 * (2 * w + n // 2 + 1))
                nc.vector.transpose(turned.rearrange("p c (b q) -> p b c q", b=GROUPS),
                                    raw[n % 2].bitcast(U32).rearrange("p b (c q) -> p b c q", q=32))\
                    .then_inc(raw_used, 1)
                dve.wait_ge(raw_used, 4 * w + n + 1)
                dst = mask[:, w, :, :].bitcast(U32).rearrange("p j (n i) -> p n j i", n=SUB)
                nc.vector.tensor_scalar(dst[:, n], turned, ONE_BIT, None, ALU.logical_shift_left)\
                    .then_inc(mask_ready, 1)

            def finish(dve, w):
                dve.wait_ge(summed_ready, 4 * w + 4)
                dve.wait_ge(summed_used, w + 1)
                nc.vector.reciprocal(rden[:], summed[:, :, F]).then_inc(rden_ready, 1)
                dve.wait_ge(rden_ready, w + 1)
                for ib in range(SUB):
                    t = X[:, w * SUB + ib, :]
                    last = nc.vector.scalar_tensor_tensor(t, summed[:, ib, 0:F], rden[:, ib:ib + 1], t,
                                                          ALU.mult, ALU.add)
                last.then_inc(summed_used, 1)

            def panel(dve, w, before, after):
                dve.wait_ge(row_loaded, 16 * w + 16)
                if layer == 0:
                    dve.wait_ge(mask_ready, 4 * w + 4)
                for j in range(PANELS):
                    if not (isinstance(w, int) and w == j == 0):
                        dve.wait_ge(m1_ready, PANELS * w + j)
                    if layer == 0 and after and j % 2:
                        turn(dve, w + 1, j // 2)
                        dve.wait_ge(mask_ready, 4 * w + 4 + j // 2 + 1)
                    for s in range(SUB):
                        last = nc.vector.tensor_scalar(gate8[:, :, s], s1_row[:, w % 2, :],
                                                       neg_s2[:, SUB * j + s:SUB * j + s + 1], ONE,
                                                       ALU.is_gt, ALU.mult)
                    last.then_inc(gates, 1)
                    if before and j == 3:
                        finish(dve, w - 1)
                    dve.wait_ge(gates, PANELS * w + j + 1)
                    dve.wait_ge(masks_used, PANELS * w + j + 1)
                    m1, m2 = (r.bitcast(U32) for r in ring[j % 2])
                    adj_w = mask[:, w, j, :].bitcast(U32)
                    nc.vector.tensor_tensor(m1, adj_w, gate8.rearrange("p i s -> p (i s)").bitcast(U32),
                                            ALU.bitwise_and).then_inc(m1_ready, 1)
                    dve.wait_ge(m1_ready, PANELS * w + j + 1)
                    nc.vector.tensor_tensor(m2, adj_w, m1, ALU.bitwise_xor).then_inc(masks_ready, 1)

            @block.vector
            def _(dve):
                dve.sem_inc(summed_used, 1)
                if layer == 0:
                    for n in range(SUB):
                        turn(dve, 0, n)
                panel(dve, 0, False, True)
                with dve.Fori(1, PANELS - 1) as w:
                    panel(dve, w, True, True)
                panel(dve, PANELS - 1, True, False)
                finish(dve, PANELS - 1)

            @block.tensor
            def _(pe):
                pe.sem_inc(masks_used, 2)
                with pe.Fori(0, PANELS) as w:
                    for j in range(PANELS):
                        wait_alone(pe, masks_ready, PANELS * w + j + 1)
                        for ib in range(SUB):
                            if j == 0:
                                wait_alone(pe, acc_scaled, 4 * w + ib + 1)
                            for s in range(SUB):
                                for m in range(2):
                                    lhs = ring[j % 2][m].bitcast(F8).rearrange("p (i s) -> p s i", s=SUB)
                                    last = nc.tensor.matmul(acc(ib, m), lhs[:, s, ib * P:ib * P + P],
                                                            V[m][:, SUB * j + s, :],
                                                            start=(j == 0 and s == 0),
                                                            stop=(j == PANELS - 1 and s == SUB - 1))
                            if j == PANELS - 1 and ib < SUB - 1:
                                last.then_inc(acc_done, 1)
                        last.then_inc(masks_used, 1)

            @block.scalar
            def _(act):
                act.sem_inc(acc_scaled, 4)
                with act.Fori(0, PANELS) as w:
                    for ib in range(SUB):
                        if ib < SUB - 1:
                            act.wait_ge(acc_done, (SUB - 1) * w + ib + 1)
                        else:
                            act.wait_ge(masks_used, PANELS * w + PANELS + 2)
                        act.wait_ge(scaled_used, 4 * w + ib + 1)
                        tile = w * SUB + ib
                        for m in range(2):
                            nc.scalar.activation(scaled[:, m, 0:F + 1], acc(ib, m)[:, 0:F + 1], ACT.Identity,
                                                 scale=AC[:, m, bass.ds(tile, 1)])
                            last = nc.scalar.activation(scaled[:, m, F + 1:VCOLS], acc(ib, m)[:, F + 1:VCOLS],
                                                        ACT.Identity, scale=AC_low[:, m, bass.ds(tile, 1)])
                        last.then_inc(acc_scaled, 1)

            @block.gpsimd
            def _(pool):
                pool.sem_inc(scaled_used, 1)

                def load(w, n):
                    pool.wait_ge(raw_used, 4 * w + n - 1)
                    load_adj(pool, w, n)

                def add(w):
                    for ib in range(SUB):
                        pool.wait_ge(acc_scaled, 4 * w + 4 + ib + 1)
                        if ib == 0:
                            pool.wait_ge(summed_used, w + 1)
                        nc.gpsimd.tensor_tensor(scaled[:, 0, :], scaled[:, 0, :], scaled[:, 1, :], ALU.add)\
                            .then_inc(added, 1)
                        pool.wait_ge(added, 4 * w + ib + 1)
                        nc.gpsimd.tensor_tensor(summed[:, ib, :], scaled[:, 0, 0:F + 1],
                                                scaled[:, 0, F + 1:VCOLS], ALU.add).then_inc(summed_ready, 1)
                        pool.wait_ge(summed_ready, 4 * w + ib + 1)
                        pool.sem_inc(scaled_used, 1)

                if layer == 0:
                    load(0, 2)
                    load(0, 3)
                    load(1, 0)
                    load(1, 1)
                    with pool.Fori(0, PANELS - 2) as w:
                        load(w + 1, 2)
                        load(w + 1, 3)
                        load(w + 2, 0)
                        load(w + 2, 1)
                        add(w)
                    load(PANELS - 1, 2)
                    load(PANELS - 1, 3)
                    add(PANELS - 2)
                    add(PANELS - 1)
                else:
                    with pool.Fori(0, PANELS) as w:
                        add(w)

        def moe_stage():
            L = "moe_"
            take = stage_buffers(mask_flat)
            W1_sb = take([E, HID])
            W2_sb = take([E * HB, F])
            Wg_sb = take([E])
            gate_b = take([3, E])
            b1_in = take([P])
            b1_col = take([E * HB])
            b2_sb = take([F])
            normed = take([SUB, F])
            normed_T = take([PW])
            hid = take([2, HB, PW])
            logits = take([SUB, E])
            top8 = take([SUB, 8])
            idx8 = take([SUB, 8], U32)
            idxf = take([SUB, 8])
            iota_f = take([E])
            wts = take([SUB, 4])
            comb = take([SUB, E])
            comb_k = take([SUB, E])
            comb_T = take([PW])
            ebias = take([2, E])
            loaded = sem(L + "loaded")
            b1_done = sem(L + "b1_done")
            b1_in_s = sem(L + "b1_in")
            iota_ready = sem(L + "iota")
            chain = sem(L + "chain")
            var_ready = sem(L + "var_ready")
            root_ready = sem(L + "root_ready")
            normed_ready = sem(L + "normed_ready")
            turned_done = sem(L + "turned_done")
            turned_in = sem(L + "turned_in")
            logits_done = sem(L + "logits_done")
            w_arg = sem(L + "w_arg")
            w_exp = sem(L + "w_exp")
            comb_ready = sem(L + "comb_ready")
            combT_done = sem(L + "combT_done")
            combT_in = sem(L + "combT_in")
            bias_done = sem(L + "bias_done")
            h_done = sem(L + "h_done")
            h_in = sem(L + "h_in")
            y_done = sem(L + "y_done")
            y_used = sem(L + "y_used")
            x_done = sem(L + "x_done")
            stored = sem(L + "stored")
            block = ctx2.enter_context(nc.Block())
            n_loads = 9

            @block.sync
            def _(sp):
                sp.dma_start(Wg_sb, Wg).then_inc(loaded, 16)
                for k, b in enumerate((bg, gbias)):
                    sp.dma_start(gate_b[:, k, :], b.rearrange("(o e) -> o e", o=1).to_broadcast((P, E)))\
                        .then_inc(loaded, 16)
                sp.dma_start(b1_in[0:E * HB, :], be1.rearrange("e (b p) -> (e b) p", b=HB)).then_inc(loaded, 16)
                sp.dma_start(b2_sb[0:E, :], be2).then_inc(loaded, 16)
                sp.dma_start(W1_sb, We1.rearrange("e d h -> d e h")).then_inc(loaded, 16)
                sp.dma_start(W2_sb.rearrange("p (e b) f -> p e b f", e=E)[:, 0:4],
                             We2.rearrange("e (b p) f -> p e b f", b=HB)[:, 0:4]).then_inc(loaded, 16)
                sp.dma_start(W2_sb.rearrange("p (e b) f -> p e b f", e=E)[:, 4:8],
                             We2.rearrange("e (b p) f -> p e b f", b=HB)[:, 4:8]).then_inc(loaded, 16)
                sp.dma_start(ebias[:, 0, :], bg.rearrange("(o e) -> o e", o=1).to_broadcast((P, E)))\
                    .then_inc(loaded, 16)
                xv = X[:].rearrange("p (c s) f -> p c (s f)", s=SUB)
                for c in range(PANELS):
                    sp.wait_ge(x_done, c + 1)
                    for g in range(GROUPS):
                        sp.dma_start(out_g[g][:, c, :], xv[32 * g:32 * g + 32, c, :]).then_inc(stored, 16)
                sp.wait_ge(stored, 16 * GROUPS * PANELS)

            @block.gpsimd
            def _(pool):
                nc.gpsimd.iota(iota_f, pattern=[[1, E]], base=0, channel_multiplier=0,
                               allow_small_or_imprecise_dtypes=True).then_inc(iota_ready, 1)

            @block.tensor
            def _(pe):
                pe.wait_ge(loaded, 16 * n_loads)
                nc.tensor.transpose(PS[:, 0, 0:E * HB], b1_in[0:E * HB, :], ident[0:E * HB, 0:E * HB])\
                    .then_inc(b1_done, 1)
                pe.wait_ge(b1_in_s, 1)
                with pe.Fori(0, PANELS) as c:
                    pe.wait_ge(normed_ready, c + 1)
                    for s in range(SUB):
                        last = nc.tensor.transpose(PS[:, 0, s * P:s * P + P], normed[:, s, :], ident[:])
                    last.then_inc(turned_done, 1)
                    pe.wait_ge(turned_in, c + 1)
                    for s in range(SUB):
                        last = nc.tensor.matmul(PS[:, 1, s * E:s * E + E], normed_T[:, s * P:s * P + P], Wg_sb,
                                                start=True, stop=True)
                    last.then_inc(logits_done, 1)

                    def hidden(e):
                        for b in range(HB):
                            pe.wait_ge(h_in, c * (E * HB) + HB * e + b + 1)
                            nc.tensor.matmul(PS[:, 2 + (HB * e + b) % 4, :], W1_sb[:, e, b * P:b * P + P],
                                             normed_T, start=True, stop=True).then_inc(h_done, 1)

                    def down(e):
                        pe.wait_ge(h_in, c * (E * HB) + 4 + HB * e + HB)
                        pe.wait_ge(y_used, c * E + e + 1)
                        for s in range(SUB):
                            for b in range(HB):
                                last = nc.tensor.matmul(PS[:, 6 + e % 2, s * F:s * F + F],
                                                        hid[:, e % 2, b, s * P:s * P + P],
                                                        W2_sb[:, HB * e + b, :],
                                                        start=(b == 0), stop=(b == HB - 1))
                        last.then_inc(y_done, 1)

                    hidden(0)
                    for e in range(1, E):
                        hidden(e)
                        if e == 1:
                            pe.wait_ge(comb_ready, c + 1)
                            for s in range(SUB):
                                last = nc.tensor.transpose(PS[0:E, 0, s * P:s * P + P], comb[:, s, :], ident[:])
                            last.then_inc(combT_done, 1)
                            pe.wait_ge(combT_in, c + 1)
                            for s in range(SUB):
                                last = nc.tensor.matmul(PS[:, 1, s * F:s * F + F], comb_T[0:E, s * P:s * P + P],
                                                        b2_sb[0:E, :], start=True, stop=True)
                            last.then_inc(bias_done, 1)
                        down(e - 1)
                    down(E - 1)

            @block.scalar
            def _(act):
                act.wait_ge(b1_done, 1)
                nc.scalar.copy(b1_col, PS[:, 0, 0:E * HB]).then_inc(b1_in_s, 1)
                act.sem_inc(h_in, 4)
                with act.Fori(0, PANELS) as c:
                    act.wait_ge(var_ready, c + 1)
                    nc.scalar.activation(rr[:, 1, :], rr[:, 0, :], ACT.Sqrt).then_inc(root_ready, 1)
                    act.wait_ge(turned_done, c + 1)
                    nc.scalar.copy(normed_T, PS[:, 0, :]).then_inc(turned_in, 1)
                    for e in range(E):
                        if e == 1:
                            act.wait_ge(w_arg, c + 1)
                            nc.scalar.activation(wts[:, :, 1], wts[:, :, 0], ACT.Exp).then_inc(w_exp, 1)
                            act.wait_ge(combT_done, c + 1)
                            nc.scalar.copy(comb_T[0:E, :], PS[0:E, 0, :]).then_inc(combT_in, 1)
                        for b in range(HB):
                            act.wait_ge(h_done, c * (E * HB) + HB * e + b + 1)
                            if b == 0:
                                act.wait_ge(y_done, c * E + e - 1) if e >= 2 else None
                            nc.scalar.activation(hid[:, e % 2, b, :], PS[:, 2 + (HB * e + b) % 4, :], ACT.Relu,
                                                 bias=b1_col[:, HB * e + b:HB * e + b + 1]).then_inc(h_in, 1)

            @block.vector
            def _(dve):
                chained = [0]

                def link(ins, base=0):
                    chained[0] += 1
                    ins.then_inc(chain, 1)
                    wait_alone(dve, chain, base + chained[0])

                dve.sem_inc(y_used, 2)
                dve.wait_ge(loaded, 16 * n_loads)
                dve.wait_ge(iota_ready, 1)
                link(nc.vector.tensor_tensor(ebias[:, 1, :], gate_b[:, 0, :], gate_b[:, 1, :], ALU.add))
                links = 26
                with dve.Fori(0, PANELS) as c:
                    base = c * links
                    start = chained[0]
                    for s in range(SUB):
                        last = nc.vector.bn_stats(stats[:, s, :], X[:, c * SUB + s, :])
                    link(last, base)
                    for s in range(SUB):
                        last = nc.vector.bn_aggr(mv[:, s, :], stats[:, s, :])
                    link(last, base)
                    nc.vector.tensor_scalar(rr[:, 0, :], mv[:, :, 1], EPS, None, ALU.add).then_inc(var_ready, 1)
                    dve.wait_ge(root_ready, c + 1)
                    link(nc.vector.reciprocal(rr[:, 2, :], rr[:, 1, :]), base)
                    link(nc.vector.tensor_tensor(rr[:, 3, :], rr[:, 2, :], rr[:, 2, :], ALU.mult), base)
                    link(nc.vector.tensor_tensor(rr[:, 3, :], rr[:, 3, :], rr[:, 0, :], ALU.mult), base)
                    link(nc.vector.tensor_scalar(rr[:, 3, :], rr[:, 3, :], -0.5, 1.5, ALU.mult, ALU.add), base)
                    link(nc.vector.tensor_tensor(rr[:, 2, :], rr[:, 2, :], rr[:, 3, :], ALU.mult), base)
                    for s in range(SUB):
                        last = nc.vector.tensor_scalar(normed[:, s, :], X[:, c * SUB + s, :], mv[:, s, 0:1],
                                                       rr[:, 2, s:s + 1], ALU.subtract, ALU.mult)
                    last.then_inc(normed_ready, 1)
                    dve.wait_ge(logits_done, c + 1)
                    link(nc.vector.tensor_tensor(logits[:], PS[:, 1, 0:SUB * E].rearrange("p (s e) -> p s e", s=SUB),
                                                 ebias[:, 1, :].rearrange("p (o e) -> p o e", o=1)
                                                 .to_broadcast((P, SUB, E)), ALU.add), base)
                    for s in range(SUB):
                        last = nc.vector.max(top8[:, s, :], logits[:, s, :])
                    link(last, base)
                    for s in range(SUB):
                        last = nc.vector.max_index(idx8[:, s, :], top8[:, s, :], logits[:, s, :])
                    link(last, base)
                    link(nc.vector.tensor_copy(idxf[:], idx8[:]), base)
                    nc.vector.tensor_tensor(wts[:, :, 0], top8[:, :, 1], top8[:, :, 0], ALU.subtract).then_inc(w_arg, 1)
                    dve.wait_ge(w_exp, c + 1)
                    link(nc.vector.tensor_scalar(wts[:, :, 0], wts[:, :, 1], 1.0, None, ALU.add), base)
                    link(nc.vector.reciprocal(wts[:, :, 2], wts[:, :, 0]), base)
                    link(nc.vector.tensor_tensor(wts[:, :, 3], wts[:, :, 1], wts[:, :, 2], ALU.mult), base)
                    for k in range(2):
                        dst = comb if k == 0 else comb_k
                        for s in range(SUB):
                            last = nc.vector.tensor_scalar(dst[:, s, :], iota_f, idxf[:, s, k:k + 1],
                                                           wts[:, s, 2 + k:3 + k], ALU.is_equal, ALU.mult)
                        link(last, base)
                    link(nc.vector.tensor_tensor(comb[:], comb[:], comb_k[:], ALU.add), base)
                    dve.sem_inc(comb_ready, 1)
                    dve.wait_ge(bias_done, c + 1)
                    x4 = X[:, bass.ds(c * SUB, SUB), :]
                    link(nc.vector.tensor_tensor(x4, x4, PS[:, 1, :].rearrange("p (s f) -> p s f", s=SUB), ALU.add), base)
                    for e in range(E):
                        dve.wait_ge(y_done, c * E + e + 1)
                        for s in range(SUB):
                            t = X[:, c * SUB + s, :]
                            last = nc.vector.scalar_tensor_tensor(t, PS[:, 6 + e % 2, s * F:s * F + F],
                                                                  comb[:, s, e:e + 1], t, ALU.mult, ALU.add)
                        link(last, base)
                        dve.sem_inc(y_used, 1)
                    dve.sem_inc(x_done, 1)
                assert chained[0] - start == links, chained[0] - start

        for stage in (lambda: node_stage(0), lambda: attention_stage(0), lambda: node_stage(1),
                      lambda: attention_stage(1), moe_stage):
            with ExitStack() as ctx2:
                stage()


_INS = ['x', 'adj', 'L0_gnn_W', 'L0_gnn_a', 'L0_ffn_weight', 'L0_ffn_bias', 'L1_gnn_W', 'L1_gnn_a', 'L1_ffn_Wg',
        'L1_ffn_bg', 'L1_ffn_bias', 'L1_ffn_W1', 'L1_ffn_b1', 'L1_ffn_W2', 'L1_ffn_b2']


def kernel(**inputs):
    import numpy as _np
    import concourse.bacc as _bacc
    from concourse import mybir as _mybir
    from concourse.bass_utils import run_bass_kernel_spmd as _run

    nc = _bacc.Bacc("TRN2", target_bir_lowering=False, num_devices=1)
    arrays, args = {}, []
    for name in _INS:
        a = _np.ascontiguousarray(inputs[name])
        arrays[f"in_{name}"] = a
        args.append(nc.dram_tensor(f"in_{name}", a.shape, _mybir.dt.from_np(a.dtype), kind="ExternalInput").ap())
    args.append(nc.dram_tensor("out_x", (4096, 128), _mybir.dt.float32, kind="ExternalOutput").ap())
    gnn_moe_kernel(nc, *args)
    r = _run(nc, [arrays], core_ids=[0])
    return r.results[0]["out_x"]
```

```python
from contextlib import ExitStack

import numpy as np

import concourse.bass as bass
from concourse import mybir

F32 = mybir.dt.float32
F16 = mybir.dt.float16
F8 = mybir.dt.float8e4
U8 = mybir.dt.uint8
U32 = mybir.dt.uint32
ALU = mybir.AluOpType
ACT = mybir.ActivationFunctionType
AX = mybir.AxisListType

N = 4096
P = 128
F = 128
TILES = N // P
GROUPS = 4
SUB = 4
PANELS = TILES // SUB
PW = SUB * P
E = 8
HID = 256
HB = HID // P
EPS = 1e-5
ALPHAS = (0.01, 0.2)
ONE_BYTE = 0x38
VCOLS = 2 * (F + 1)
V_SCALE = 256.0
LOW = 2048.0
SX, SW, SH = 4.0, 64.0, 16.0


def gnn_moe_kernel(nc, x, adj, W0, a0, Wf, bf, W1, a1, Wg, bg, gbias, We1, be1, We2, be2, out):
    x_g = x.rearrange("(g c q s) f -> g q c (s f)", g=GROUPS, c=PANELS, q=32, s=SUB)
    out_g = out.rearrange("(g c q s) f -> g q c (s f)", g=GROUPS, c=PANELS, q=32, s=SUB)
    adj_g = adj.rearrange("(b c q s) (g k) -> c s g q b k", b=GROUPS, c=PANELS, q=32, s=SUB, g=GROUPS)

    with ExitStack() as ctx:
        def sb(name, shape, dt):
            return ctx.enter_context(nc.sbuf_tensor(name, shape, dt))

        def wait_alone(eng, semaphore, value):
            eng.wait_ge(semaphore, value)
            eng.sem_inc(passed[str(eng.engine)], 1)

        def sem(name):
            return ctx.enter_context(nc.semaphore(name))

        passed = {str(e.engine): sem(f"passed_{n}") for n, e in (("pe", nc.tensor), ("pool", nc.gpsimd))}
        s1_rows = nc.dram_tensor("s1_rows", [2, TILES, P], F32)

        mask = sb("mask", [P, PANELS, PANELS, PW * SUB], U8)
        X = sb("X", [P, TILES, F], F32)
        V = [sb(f"V{m}", [P, TILES, VCOLS], F16) for m in range(2)]
        val = V[1][:].rearrange("p t c -> p (t c)").bitcast(F32).rearrange("p (t c) -> p t c", t=TILES)[:, :, 0:F]
        s1_row = sb("s1_row", [P, 2, PW], F32)
        ident = sb("ident", [P, P], F32)
        S12 = sb("S12", [P, 2, TILES], F32)
        neg_s2 = sb("neg_s2", [P, TILES], F32)
        AC = sb("AC", [P, 2, TILES], F32)
        BD = sb("BD", [P, 2, TILES], F32)
        den_high = sb("den_high", [P, 2, TILES], F16)
        den_low = sb("den_low", [P, 2, TILES], F16)
        smax = sb("smax", [P, 2], F32)
        mean = sb("mean", [P, TILES], F32)
        rstd = sb("rstd", [P, TILES], F32)
        rden = sb("rden", [P, SUB], F32)

        def at(buf, start, shape, dt, size):
            n = int(np.prod(shape))
            flat = buf[:, start:start + n * size].bitcast(dt)
            if len(shape) == 1:
                return flat
            names = "abcd"[:len(shape)]
            return flat.rearrange(f"p ({' '.join(names)}) -> p {' '.join(names)}",
                                  **{k: v for k, v in zip(names, shape)})

        raw = sb("raw", [P, 2, GROUPS, 1024], U8)
        turned = sb("turned", [P, PANELS, P], U32)
        work = sb("work", [P, 20640], U8)
        gate8 = [at(work, 2048 * n, [PW, SUB], U8, 1) for n in range(2)]
        ring = [[at(work, 4096 + 4096 * n + 2048 * m, [PW * SUB], U8, 1) for m in range(2)] for n in range(2)]
        scaled = [at(work, 12288 + 2064 * n, [2, VCOLS], F32, 4) for n in range(2)]
        summed = at(work, 16416, [SUB, VCOLS], F32, 4)
        product = [at(work, 12288 + 2048 * m, [SUB, F], F32, 4) for m in range(2)]

        def carve(buf):
            o = [0]

            def take(shape, dt=F32, size=4):
                r = at(buf, o[0], shape, dt, size)
                o[0] += int(np.prod(shape)) * size
                return r
            return take

        PS = ctx.enter_context(nc.psum_tensor("PS", [P, 8, 512], F32))

        def acc(ib, m):
            return PS[:, 2 * ib + m, 0:VCOLS]

        raw_ready = [sem(f"raw_ready{n}") for n in range(2)]
        raw_used = sem("raw_used")
        mask_ready = sem("mask_ready")

        def load_adj(pool, w, n):
            if not (isinstance(w, int) and 4 * w + n < 2):
                pool.wait_ge(raw_used, 4 * w + n - 1)
            for g in range(GROUPS):
                pool.dma_start(raw[32 * g:32 * g + 32, n % 2], adj_g[w, n, g], max_dma_last_dim=4096)\
                    .then_inc(raw_ready[n % 2], 16)

        def turn(dve, w, n):
            if not (isinstance(w, int) and 4 * w + n == 0):
                dve.wait_ge(mask_ready, 4 * w + n)
            dve.wait_ge(raw_ready[n % 2], 64 * (2 * w + n // 2 + 1))
            nc.vector.transpose(turned[:].rearrange("p c (b q) -> p b c q", b=GROUPS),
                                raw[:, n % 2].bitcast(U32).rearrange("p b (c q) -> p b c q", q=32))\
                .then_inc(raw_used, 1)

        def settle(act, w, n):
            act.wait_ge(raw_used, 4 * w + n + 1)
            nc.scalar.mul(mask[:, w, :, 4 * P * n:4 * P * n + 4 * P],
                          turned[:].rearrange("p c i -> p (c i)").bitcast(U8).rearrange("p (c i) -> p c i", c=PANELS),
                          float(ONE_BYTE)).then_inc(mask_ready, 1)

        def norm_stats(dve, tag, stats, tmp, root_ready, var_ready):
            chain = sem(tag + "_stats_chain")
            n = [0]

            def link(ins):
                n[0] += 1
                ins.then_inc(chain, 1)
                dve.wait_ge(chain, n[0])

            for t in range(TILES):
                last = nc.vector.bn_stats(stats[:, t, :], X[:, t, :])
            link(last)
            nc.vector.tensor_tensor(mean[:], stats[:, :, 1], stats[:, :, 4], ALU.add)
            nc.vector.tensor_tensor(tmp[:, 1, :], stats[:, :, 2], stats[:, :, 5], ALU.add)
            link(nc.vector.tensor_tensor(tmp[:, 0, :], stats[:, :, 1], stats[:, :, 4], ALU.subtract))
            nc.vector.tensor_scalar(mean[:], mean[:], 0.5, None, ALU.mult)
            link(nc.vector.tensor_tensor(tmp[:, 0, :], tmp[:, 0, :], tmp[:, 0, :], ALU.mult))
            link(nc.vector.scalar_tensor_tensor(tmp[:, 0, :], tmp[:, 0, :], F / 4.0, tmp[:, 1, :], ALU.mult, ALU.add))
            nc.vector.tensor_scalar(tmp[:, 0, :], tmp[:, 0, :], 1.0 / F, EPS, ALU.mult, ALU.add).then_inc(var_ready, 1)
            dve.wait_ge(root_ready, 1)
            link(nc.vector.reciprocal(rstd[:], tmp[:, 2, :]))
            link(nc.vector.tensor_tensor(tmp[:, 3, :], rstd[:], rstd[:], ALU.mult))
            link(nc.vector.tensor_tensor(tmp[:, 3, :], tmp[:, 3, :], tmp[:, 0, :], ALU.mult))
            link(nc.vector.tensor_scalar(tmp[:, 3, :], tmp[:, 3, :], -0.5, 1.5, ALU.mult, ALU.add))
            link(nc.vector.tensor_tensor(rstd[:], rstd[:], tmp[:, 3, :], ALU.mult))

        def normalise(dst, t):
            return nc.vector.tensor_scalar(dst, X[:, t, :], mean[:, t:t + 1], rstd[:, t:t + 1],
                                           ALU.subtract, ALU.mult)

        def node_stage(layer):
            L = f"n{layer}_"
            take = carve(work)
            normed = [s1_row[:, n, :].rearrange("p (s f) -> p s f", s=SUB) for n in range(2)]
            normed_T = [take([PW]) for _ in range(2)]
            W_ext = take([F + 2])
            Wf_T = take([F])
            bias_row = take([F])
            W_T = take([F])
            Wf_in = take([F])
            a_cols = take([2])
            s1_T = take([P])
            stats = [take([TILES, 6]) for _ in range(1 + layer)]
            tmp = [take([4, TILES]) for _ in range(1 + layer)]
            warg = take([3, TILES])
            den_rest = take([2, TILES])
            W, a, alpha = ((W0, a0, ALPHAS[0]), (W1, a1, ALPHAS[1]))[layer]

            x_loaded = sem(L + "x_loaded")
            loaded = sem(L + "loaded")
            ident_ready = sem(L + "ident_ready")
            weights_T = sem(L + "weights_T")
            weights_in = sem(L + "weights_in")
            wa_done = sem(L + "wa_done")
            wa_in = sem(L + "wa_in")
            var_ready = [sem(f"{L}var_ready{k}") for k in range(1 + layer)]
            root_ready = [sem(f"{L}root_ready{k}") for k in range(1 + layer)]
            normed_ready = sem(L + "normed_ready")
            turned_done = sem(L + "turned_done")
            turned_in = sem(L + "turned_in")
            prod_done = sem(L + "prod_done")
            x_added = sem(L + "x_added")
            s12_in = sem(L + "s12_in")
            val_in = sem(L + "val_in")
            bias_in = sem(L + "bias_in")
            pmax = sem(L + "pmax")
            allmax = sem(L + "allmax")
            warg0 = sem(L + "warg0")
            args_ready = sem(L + "args_ready")
            exps_ready = sem(L + "exps_ready")
            factors_ready = sem(L + "factors_ready")
            den_high_in = sem(L + "den_high_in")
            den_rest_ready = sem(L + "den_rest_ready")
            den_low_in = sem(L + "den_low_in")
            den_cols = sem(L + "den_cols")
            s1T_done = sem(L + "s1T_done")
            s1T_in = sem(L + "s1T_in")
            rows_out = sem(L + "rows_out")

            chunks = [(k, c) for k in range(1 + layer) for c in range(PANELS)]
            gnn = PANELS * layer
            n_loads = 4 if layer else 2
            block = ctx2.enter_context(nc.Block())

            def bank_T(q):
                return PS[:, q % 2, :]

            def products(q):
                b = 2 + 2 * (q % 2)
                return PS[:, b:b + 2, :].rearrange("p b (h f) -> p (b h) f", h=2)

            @block.sync
            def _(sp):
                if layer == 0:
                    for g in range(GROUPS):
                        sp.dma_start(X[32 * g:32 * g + 32].rearrange("p (c s) f -> p c (s f)", s=SUB), x_g[g])\
                            .then_inc(x_loaded, 16)
                sp.dma_start(W_ext[:, 0:F], W).then_inc(loaded, 16)
                with nc.allow_non_contiguous_dma(reason="256 scalars"):
                    sp.dma_start(a_cols, a.rearrange("(c p) one -> p (c one)", c=2)).then_inc(loaded, 16)
                if layer == 1:
                    sp.dma_start(Wf_in, Wf).then_inc(loaded, 16)
                    sp.dma_start(bias_row, bf.rearrange("(o f) -> o f", o=1).to_broadcast((P, F)))\
                        .then_inc(loaded, 16)
                sp.wait_ge(s1T_in, 1)
                sp.dma_start(s1_rows[layer], s1_T[0:TILES, :]).then_inc(rows_out, 16)
                sp.wait_ge(rows_out, 16)

            @block.gpsimd
            def _(pool):
                if layer == 0:
                    load_adj(pool, 0, 0)
                    load_adj(pool, 0, 1)
                    nc.gpsimd.memset(ident[:], 0.0).then_inc(ident_ready, 1)
                    pool.wait_ge(ident_ready, 1)
                    nc.gpsimd.affine_select(out=ident[:], in_=ident[:], compare_op=ALU.not_equal, fill=1.0,
                                            base=0, pattern=[[-1, P]], channel_multiplier=1).then_inc(ident_ready, 1)
                    load_adj(pool, 0, 2)
                    load_adj(pool, 0, 3)
                    load_adj(pool, 1, 0)
                    load_adj(pool, 1, 1)
                else:
                    pool.wait_ge(loaded, 16 * n_loads)
                    for c in range(PANELS):
                        pool.wait_ge(normed_ready, c + 1)
                        x4 = X[:, SUB * c:SUB * c + SUB, :]
                        nc.gpsimd.tensor_tensor(x4, x4, bias_row.rearrange("p (o f) -> p o f", o=1)
                                                .to_broadcast((P, SUB, F)), ALU.add).then_inc(bias_in, 1)
                pool.wait_ge(pmax, 1)
                nc.gpsimd.partition_all_reduce(smax[:, 1:2], smax[:, 0:1], P, bass.bass_isa.ReduceOp.max)\
                    .then_inc(allmax, 1)

            @block.tensor
            def _(pe):
                if layer == 0:
                    pe.wait_ge(ident_ready, 2)
                pe.wait_ge(loaded, 16 * n_loads)
                last = nc.tensor.transpose(PS[:, 6, 0:P], W_ext[:, 0:F], ident[:])
                if layer == 1:
                    last = nc.tensor.transpose(PS[:, 6, P:2 * P], Wf_in, ident[:])
                last.then_inc(weights_T, 1)
                pe.wait_ge(weights_in, 1)
                nc.tensor.matmul(PS[:, 7, 0:2], W_T, a_cols, start=True, stop=True).then_inc(wa_done, 1)
                pe.wait_ge(wa_in, 1)

                def to_T(q):
                    pe.wait_ge(normed_ready, q + 1)
                    if q >= 2:
                        pe.wait_ge(turned_in, q - 1)
                    for s in range(SUB):
                        last = nc.tensor.transpose(bank_T(q)[:, s * P:s * P + P], normed[q % 2][:, s, :], ident[:])
                    last.then_inc(turned_done, 1)

                to_T(0)
                for q, (k, c) in enumerate(chunks):
                    if q + 1 < len(chunks):
                        if q + 1 != gnn or not layer:
                            to_T(q + 1)
                    pe.wait_ge(turned_in, q + 1)
                    if q - 2 >= gnn:
                        pe.wait_ge(s12_in, q - 2 - gnn + 1)
                        (pe.wait_ge(val_in, q - 2 - gnn + 1) if layer else pe.wait_ge(x_added, q - 1))
                    elif q >= 2:
                        pe.wait_ge(x_added, q - 1)
                    rhs = Wf_T if q < gnn else W_ext
                    for s in range(SUB):
                        last = nc.tensor.matmul(products(q)[:, s, 0:rhs.shape[1]], normed_T[q % 2][:, s * P:s * P + P],
                                                rhs, start=True, stop=True)
                    last.then_inc(prod_done, 1)
                    if q + 1 == gnn and layer:
                        to_T(q + 1)
                pe.wait_ge(s12_in, PANELS)
                nc.tensor.transpose(PS[0:TILES, 6, 0:P], S12[:, 0, :], ident[:]).then_inc(s1T_done, 1)

            def outs(act, q):
                c = q - gnn
                act.wait_ge(prod_done, q + 1)
                if layer == 1:
                    nc.scalar.copy(val[:, SUB * c:SUB * c + SUB, :], products(q)[:, :, 0:F]).then_inc(val_in, 1)
                nc.scalar.copy(S12[:, :, SUB * c:SUB * c + SUB].rearrange("p k s -> p s k"),
                               products(q)[:, :, F:F + 2]).then_inc(s12_in, 1)

            @block.scalar
            def _(act):
                act.wait_ge(weights_T, 1)
                if layer == 1:
                    nc.scalar.copy(Wf_T, PS[:, 6, P:2 * P])
                nc.scalar.copy(W_T, PS[:, 6, 0:P]).then_inc(weights_in, 1)
                act.wait_ge(wa_done, 1)
                nc.scalar.copy(W_ext[:, F:F + 2], PS[:, 7, 0:2]).then_inc(wa_in, 1)
                for k in range(1 + layer):
                    act.wait_ge(var_ready[k], 1)
                    nc.scalar.activation(tmp[k][:, 2, :], tmp[k][:, 0, :], ACT.Sqrt).then_inc(root_ready[k], 1)
                    if layer == 0:
                        settle(act, 0, 0)
                    for c in range(PANELS):
                        q = PANELS * k + c
                        act.wait_ge(turned_done, q + 1)
                        if q >= 2:
                            act.wait_ge(prod_done, q - 1)
                        nc.scalar.copy(normed_T[q % 2], bank_T(q)).then_inc(turned_in, 1)
                        if layer == 0:
                            nc.scalar.copy(val[:, SUB * c:SUB * c + SUB, :], normed[c % 2]).then_inc(val_in, 1)
                        if k == layer and c:
                            outs(act, q - 1)
                        if layer == 0 and c in (1, 3, 5):
                            settle(act, 0, (c + 1) // 2)
                outs(act, len(chunks) - 1)
                act.wait_ge(s1T_done, 1)
                nc.scalar.copy(s1_T[0:TILES, :], PS[0:TILES, 6, 0:P]).then_inc(s1T_in, 1)
                act.wait_ge(args_ready, 1)
                nc.scalar.activation(BD[:, 0, :], warg[:, 2, :], ACT.Exp).then_inc(exps_ready, 1)
                nc.scalar.activation(BD[:, 1, :], warg[:, 2, :], ACT.Exp, scale=alpha).then_inc(exps_ready, 1)
                nc.scalar.activation(AC[:], warg[:, 0:2, :], ACT.Exp).then_inc(exps_ready, 1)
                act.wait_ge(factors_ready, 1)
                nc.scalar.copy(den_high[:], BD[:]).then_inc(den_high_in, 1)
                act.wait_ge(den_rest_ready, 1)
                nc.scalar.mul(den_low[:], den_rest[:], LOW).then_inc(den_low_in, 1)
                act.wait_ge(den_low_in, 1)
                nc.scalar.copy(V[0][:, :, F], den_high[:, 0, :])
                nc.scalar.copy(V[0][:, :, 2 * F + 1], den_low[:, 0, :]).then_inc(den_cols, 1)

            @block.vector
            def _(dve):
                if layer == 0:
                    dve.wait_ge(x_loaded, 16 * GROUPS)

                def add(q):
                    c = q % PANELS
                    dve.wait_ge(prod_done, q + 1)
                    if layer == 1:
                        dve.wait_ge(bias_in, c + 1)
                    else:
                        dve.wait_ge(s12_in, c + 1)
                    x4 = X[:, SUB * c:SUB * c + SUB, :]
                    nc.vector.tensor_tensor(x4, x4, products(q)[:, :, 0:F], ALU.add).then_inc(x_added, 1)

                for k in range(1 + layer):
                    if k:
                        dve.wait_ge(x_added, PANELS)
                    norm_stats(dve, f"{L}{k}", stats[k], tmp[k], root_ready[k], var_ready[k])
                    adds = k < layer or layer == 0
                    for c in range(PANELS):
                        q = PANELS * k + c
                        if q >= 2:
                            dve.wait_ge(turned_done, q - 1)
                            if layer == 0:
                                dve.wait_ge(val_in, q - 1)
                        for s in range(SUB):
                            last = normalise(normed[q % 2][:, s, :], SUB * c + s)
                        last.then_inc(normed_ready, 1)
                        if layer == 0 and c % 2 == 0:
                            turn(dve, 0, c // 2)
                        if adds and c >= 2:
                            add(q - 2)
                    if adds:
                        add(PANELS * k + PANELS - 2)
                        add(PANELS * k + PANELS - 1)
                dve.wait_ge(s12_in, PANELS)
                nc.vector.tensor_reduce(smax[:, 0:1], S12[:, 1, :], AX.X, ALU.max).then_inc(pmax, 1)
                nc.vector.tensor_scalar(neg_s2[:], S12[:, 1, :], -1.0, None, ALU.mult)
                dve.wait_ge(allmax, 1)
                nc.vector.tensor_scalar(warg[:, 2, :], S12[:, 1, :], smax[:, 1:2], None, ALU.subtract)
                nc.vector.tensor_scalar(warg[:, 0, :], S12[:, 0, :], smax[:, 1:2], 1.0 - alpha,
                                        ALU.add, ALU.mult).then_inc(warg0, 1)
                dve.wait_ge(warg0, 1)
                nc.vector.tensor_scalar(warg[:, 1, :], warg[:, 0, :], -1.0, 0.0, ALU.mult, ALU.min).then_inc(warg0, 1)
                dve.wait_ge(warg0, 2)
                nc.vector.tensor_scalar(warg[:, 0, :], warg[:, 0, :], 0.0, None, ALU.min).then_inc(args_ready, 1)
                dve.wait_ge(exps_ready, 2)
                nc.vector.tensor_scalar(BD[:], BD[:], V_SCALE, None, ALU.mult).then_inc(factors_ready, 1)
                dve.wait_ge(factors_ready, 1)
                dve.wait_ge(den_high_in, 1)
                nc.vector.tensor_tensor(den_rest[:], BD[:], den_high[:], ALU.subtract).then_inc(den_rest_ready, 1)

        def attention_stage(layer):
            L = f"a{layer}_"
            row_loaded = sem(L + "row_loaded")
            product_ready = sem(L + "product_ready")
            v_high = sem(L + "v_high")
            v_rest = sem(L + "v_rest")
            v_low = sem(L + "v_low")
            den_in = sem(L + "den_in")
            gates = sem(L + "gates")
            m1_ready = sem(L + "m1_ready")
            masks_ready = sem(L + "masks_ready")
            masks_used = sem(L + "masks_used")
            acc_done = sem(L + "acc_done")
            acc_out = sem(L + "acc_out")
            scaled_used = sem(L + "scaled_used")
            lows_scaled = sem(L + "lows_scaled")
            summed_ready = sem(L + "summed_ready")
            rden_ready = sem(L + "rden_ready")
            summed_used = sem(L + "summed_used")
            block = ctx2.enter_context(nc.Block())

            def row(w):
                return s1_rows[layer, bass.ds(w * SUB, SUB), :].rearrange("(o s) p -> o (s p)", o=1)\
                    .to_broadcast((P, PW))

            @block.sync
            def _(sp):
                sp.dma_start(s1_row[:, 0, :], row(0)).then_inc(row_loaded, 16)
                sp.wait_ge(row_loaded, 16)
                sp.dma_start(s1_row[:, 1, :], row(1)).then_inc(row_loaded, 16)
                with sp.Fori(2, PANELS) as w:
                    sp.wait_ge(row_loaded, 16 * w)
                    sp.wait_ge(gates, PANELS * (w - 1))
                    sp.dma_start(s1_row[:, w % 2, :], row(w)).then_inc(row_loaded, 16)
                if layer == 1:
                    sp.dma_start(W1_in, We1.rearrange("e d h -> d e h")).then_inc(experts_loaded, 16)
                    for h in range(2):
                        sp.dma_start(W2_in.rearrange("p (e b) f -> p e b f", e=E)[:, 4 * h:4 * h + 4],
                                     We2.rearrange("e (b p) f -> p e b f", b=HB)[:, 4 * h:4 * h + 4])\
                            .then_inc(experts_loaded, 16)

            def finish(dve, w):
                dve.wait_ge(summed_ready, w + 1)
                dve.wait_ge(summed_used, w + 1)
                nc.vector.reciprocal(rden[:], summed[:, :, F]).then_inc(rden_ready, 1)
                dve.wait_ge(rden_ready, w + 1)
                for ib in range(SUB):
                    t = X[:, w * SUB + ib, :]
                    last = nc.vector.scalar_tensor_tensor(t, summed[:, ib, 0:F], rden[:, ib:ib + 1], t,
                                                          ALU.mult, ALU.add)
                last.then_inc(summed_used, 1)

            def gate(w, j, half):
                for s in range(2 * half, 2 * half + 2):
                    last = nc.vector.tensor_scalar(gate8[j % 2][:, :, s], s1_row[:, w % 2, :],
                                                   neg_s2[:, SUB * j + s:SUB * j + s + 1], float(ONE_BYTE),
                                                   ALU.is_gt, ALU.mult)
                return last

            def panel(dve, w, first, final):
                for j in range(PANELS):
                    if first:
                        for m in range(2):
                            if j:
                                dve.wait_ge(v_low, 2 * j - 1 + m)
                            factor = BD[:, m, SUB * j:SUB * j + SUB].rearrange("p (s o) -> p s o", o=1)\
                                .to_broadcast((P, SUB, F))
                            nc.vector.tensor_tensor(product[m], val[:, SUB * j:SUB * j + SUB, :], factor, ALU.mult)\
                                .then_inc(product_ready, 1)
                    if layer == 0 and j == 0:
                        dve.wait_ge(mask_ready, 4 * w + 4)
                    dve.wait_ge(gates, PANELS * w + j + 1)
                    dve.wait_ge(masks_used, PANELS * w + j + 1)
                    m1, m2 = (r.bitcast(U32) for r in ring[j % 2])
                    adj_w = mask[:, w, j, :].bitcast(U32)
                    nc.vector.tensor_tensor(m1, adj_w, gate8[j % 2].rearrange("p i s -> p (i s)").bitcast(U32),
                                            ALU.bitwise_and).then_inc(m1_ready, 1)
                    more = not (final and j == PANELS - 1)
                    nw, nj = (w, j + 1) if j < PANELS - 1 else (w + 1, 0)
                    if more:
                        if nj == 0:
                            dve.wait_ge(row_loaded, 16 * nw + 16)
                        if not (first and j == 0):
                            dve.wait_ge(m1_ready, PANELS * w + j)
                        gate(nw, nj, 0)
                    if first:
                        for m in range(2):
                            dve.wait_ge(v_high, 2 * j + m + 1)
                            tiles = V[m][:, SUB * j:SUB * j + SUB, 0:F]
                            nc.vector.tensor_tensor(product[m], product[m], tiles, ALU.subtract).then_inc(v_rest, 1)
                    dve.wait_ge(m1_ready, PANELS * w + j + 1)
                    nc.vector.tensor_tensor(m2, adj_w, m1, ALU.bitwise_xor).then_inc(masks_ready, 1)
                    if layer == 0 and not final and j % 2 == 0:
                        turn(dve, w + 1, j // 2)
                    if more:
                        gate(nw, nj, 1).then_inc(gates, 1)
                    if not first and j == 3:
                        finish(dve, w - 1)

            @block.vector
            def _(dve):
                dve.sem_inc(summed_used, 1)
                dve.wait_ge(row_loaded, 16)
                gate(0, 0, 0)
                gate(0, 0, 1).then_inc(gates, 1)
                panel(dve, 0, True, False)
                with dve.Fori(1, PANELS - 1) as w:
                    panel(dve, w, False, False)
                panel(dve, PANELS - 1, False, True)
                finish(dve, PANELS - 1)

            @block.tensor
            def _(pe):
                pe.sem_inc(masks_used, 2)
                with pe.Fori(0, PANELS) as w:
                    for j in range(PANELS):
                        pe.wait_ge(v_low, 2 * j + 2)
                        pe.wait_ge(den_in, j + 1)
                        wait_alone(pe, masks_ready, PANELS * w + j + 1)
                        for ib in range(SUB):
                            if j == 0:
                                wait_alone(pe, acc_out, 4 * w + ib + 1)
                            for s in range(SUB):
                                for m in range(2):
                                    lhs = ring[j % 2][m].bitcast(F8).rearrange("p (i s) -> p s i", s=SUB)
                                    last = nc.tensor.matmul(acc(ib, m), lhs[:, s, ib * P:ib * P + P],
                                                            V[m][:, SUB * j + s, :],
                                                            start=(j == 0 and s == 0),
                                                            stop=(j == PANELS - 1 and s == SUB - 1))
                            if j == PANELS - 1 and ib < SUB - 1:
                                last.then_inc(acc_done, 1)
                        last.then_inc(masks_used, 1)

            def drain_sums(act, w):
                for ib in range(SUB):
                    if ib < SUB - 1:
                        act.wait_ge(acc_done, (SUB - 1) * w + ib + 1)
                    else:
                        act.wait_ge(masks_used, PANELS * w + PANELS + 2)
                    act.wait_ge(scaled_used, 4 * w + ib + 1)
                    for m in range(2):
                        last = nc.scalar.activation(scaled[ib % 2][:, m, :], acc(ib, m), ACT.Identity,
                                                    scale=AC[:, m, bass.ds(w * SUB + ib, 1)])
                    last.then_inc(acc_out, 1)

            @block.scalar
            def _(act):
                act.sem_inc(acc_out, 4)
                for c in range(PANELS):
                    tiles = [V[m][:, SUB * c:SUB * c + SUB, :] for m in range(2)]
                    for m in range(2):
                        act.wait_ge(product_ready, 2 * c + 1 + m)
                        nc.scalar.copy(tiles[m][:, :, 0:F], product[m]).then_inc(v_high, 1)
                    for m in range(2):
                        act.wait_ge(v_rest, 2 * c + m + 1)
                        nc.scalar.mul(tiles[m][:, :, F + 1:2 * F + 1], product[m], LOW).then_inc(v_low, 1)
                    if layer == 0 and c % 2 == 0:
                        settle(act, 1, c // 2)
                act.wait_ge(v_low, 2 * PANELS)
                drain_sums(act, 0)
                with act.Fori(1, PANELS - 1) as w:
                    if layer == 0:
                        for n in range(SUB):
                            settle(act, w + 1, n)
                    drain_sums(act, w)
                drain_sums(act, PANELS - 1)

            @block.gpsimd
            def _(pool):
                pool.sem_inc(scaled_used, 2)

                def den_columns(c):
                    pool.wait_ge(product_ready, 2 * c + 2)
                    nc.gpsimd.tensor_copy(V[1][:, SUB * c:SUB * c + SUB, F], den_high[:, 1, SUB * c:SUB * c + SUB])
                    nc.gpsimd.tensor_copy(V[1][:, SUB * c:SUB * c + SUB, 2 * F + 1],
                                          den_low[:, 1, SUB * c:SUB * c + SUB]).then_inc(den_in, 1)

                def add(w):
                    for ib in range(SUB):
                        pool.wait_ge(acc_out, 4 * w + 4 + ib + 1)
                        if ib == 0:
                            pool.wait_ge(summed_used, w + 1)
                        nc.gpsimd.tensor_tensor(summed[:, ib, :], scaled[ib % 2][:, 0, :], scaled[ib % 2][:, 1, :],
                                                ALU.add).then_inc(scaled_used, 1)
                    wait_alone(pool, scaled_used, 4 * w + 6)
                    lows = summed[:, :, F + 1:VCOLS]
                    nc.gpsimd.tensor_scalar(lows, lows, 1.0 / LOW, 0.0, ALU.mult, ALU.add).then_inc(lows_scaled, 1)
                    pool.wait_ge(lows_scaled, w + 1)
                    nc.gpsimd.tensor_tensor(summed[:, :, 0:F + 1], summed[:, :, 0:F + 1], lows, ALU.add)\
                        .then_inc(summed_ready, 1)

                for c in range(PANELS):
                    den_columns(c)
                    if layer == 0 and c % 2:
                        load_adj(pool, 1 + (2 + c // 2) // 4, (2 + c // 2) % 4)
                pool.wait_ge(v_low, 2 * PANELS)
                if layer == 0:
                    add(0)
                    with pool.Fori(1, PANELS - 2) as w:
                        load_adj(pool, w + 1, 2)
                        load_adj(pool, w + 1, 3)
                        load_adj(pool, w + 2, 0)
                        load_adj(pool, w + 2, 1)
                        add(w)
                    load_adj(pool, PANELS - 1, 2)
                    load_adj(pool, PANELS - 1, 3)
                    add(PANELS - 2)
                    add(PANELS - 1)
                else:
                    with pool.Fori(0, PANELS) as w:
                        add(w)

        take = carve(mask[:].rearrange("p a b c -> p (a b c)"))
        PARTS = ((0, 0), (0, 1), (1, 0))
        W1_in = take([E, HID])
        W2_in = take([E * HB, F])
        W1_p = [take([E, HID], F16, 2) for _ in range(2)]
        W2_p = [take([E * HB, F], F16, 2) for _ in range(2)]
        xT = [take([TILES, P], F16, 2) for _ in range(2)]
        b1_col = take([E * HB])
        comb = take([TILES, E])
        experts_loaded = sem("experts_loaded")

        def gate_stage():
            L = "g_"
            Wg_in = take([E])
            Wg_p = [take([E], F16, 2) for _ in range(2)]
            gate_b = take([3, E])
            b1_in = take([P])
            b2_in = take([F])
            b2_s = take([F])
            normed = [take([SUB, F]) for _ in range(2)]
            logits = take([TILES, E])
            top8 = take([TILES, 8])
            idx8 = take([TILES, 8], U32)
            idxf = take([TILES, 8])
            iota_f = take([E])
            wts = take([4, TILES])
            comb_k = take([2, TILES, E])
            comb_T = take([TILES, P])
            stats = take([TILES, 6])
            tmp = take([4, TILES])
            loaded = sem(L + "loaded")
            b1_done = sem(L + "b1_done")
            high_in = sem(L + "high_in")
            low_in = sem(L + "low_in")
            b1_in_s = sem(L + "b1_in")
            iota_ready = sem(L + "iota_ready")
            chain = sem(L + "chain")
            var_ready = sem(L + "var_ready")
            root_ready = sem(L + "root_ready")
            normed_ready = sem(L + "normed_ready")
            turned_done = sem(L + "turned_done")
            xT_high = sem(L + "xT_high")
            xT_low = sem(L + "xT_low")
            logits_done = sem(L + "logits_done")
            w_arg = sem(L + "w_arg")
            w_exp = sem(L + "w_exp")
            comb_ready = sem(L + "comb_ready")
            combT_done = sem(L + "combT_done")
            combT_in = sem(L + "combT_in")
            bias_done = sem(L + "bias_done")
            bias_added = sem(L + "bias_added")
            n_loads = 5
            block = ctx2.enter_context(nc.Block())
            weights = ((Wg_in, Wg_p), (W1_in, W1_p), (W2_in, W2_p))

            @block.sync
            def _(sp):
                sp.dma_start(Wg_in, Wg).then_inc(loaded, 16)
                for k, b in enumerate((bg, gbias)):
                    sp.dma_start(gate_b[:, k, :], b.rearrange("(o e) -> o e", o=1).to_broadcast((P, E)))\
                        .then_inc(loaded, 16)
                sp.dma_start(b1_in[0:E * HB, :], be1.rearrange("e (b p) -> (e b) p", b=HB)).then_inc(loaded, 16)
                sp.dma_start(b2_in[0:E, :], be2).then_inc(loaded, 16)

            @block.gpsimd
            def _(pool):
                nc.gpsimd.iota(iota_f, pattern=[[1, E]], base=0, channel_multiplier=0,
                               allow_small_or_imprecise_dtypes=True).then_inc(iota_ready, 1)

            @block.tensor
            def _(pe):
                pe.wait_ge(loaded, 16 * n_loads)
                nc.tensor.transpose(PS[:, 6, 0:E * HB], b1_in[0:E * HB, :], ident[0:E * HB, 0:E * HB])\
                    .then_inc(b1_done, 1)

                def gate_logits(c):
                    pe.wait_ge(xT_low, c + 1)
                    for s in range(SUB):
                        t = SUB * c + s
                        for n, (x_part, w_part) in enumerate(PARTS):
                            last = nc.tensor.matmul(PS[:, 7, t * E:t * E + E], xT[x_part][:, t, :], Wg_p[w_part],
                                                    start=(n == 0), stop=(n == len(PARTS) - 1))
                    last.then_inc(logits_done, 1)

                for c in range(PANELS):
                    pe.wait_ge(normed_ready, c + 1)
                    if c >= 2:
                        pe.wait_ge(xT_low, c - 1)
                    for s in range(SUB):
                        last = nc.tensor.transpose(PS[:, c % 2, s * P:s * P + P], normed[c % 2][:, s, :], ident[:])
                    last.then_inc(turned_done, 1)
                    if c == 0:
                        pe.wait_ge(low_in, 1)
                    else:
                        gate_logits(c - 1)
                gate_logits(PANELS - 1)

                pe.wait_ge(comb_ready, 1)
                for c in range(PANELS + 1):
                    if c < PANELS:
                        if c >= 2:
                            pe.wait_ge(combT_in, c - 1)
                        for s in range(SUB):
                            last = nc.tensor.transpose(PS[0:E, c % 2, s * P:s * P + P], comb[:, SUB * c + s, :],
                                                       ident[:])
                        last.then_inc(combT_done, 1)
                    if c:
                        pe.wait_ge(combT_in, c)
                        if c > 2:
                            pe.wait_ge(bias_added, c - 2)
                        for s in range(SUB):
                            last = nc.tensor.matmul(PS[:, 2 + (c - 1) % 2, s * F:s * F + F],
                                                    comb_T[0:E, SUB * (c - 1) + s, :], b2_s[0:E, :],
                                                    start=True, stop=True)
                        last.then_inc(bias_done, 1)

            @block.scalar
            def _(act):
                act.wait_ge(loaded, 16 * n_loads)
                nc.scalar.mul(Wg_p[0], Wg_in, SW).then_inc(high_in, 1)
                nc.scalar.mul(b2_s[0:E, :], b2_in[0:E, :], SW * SH).then_inc(high_in, 1)
                act.wait_ge(b1_done, 1)
                nc.scalar.mul(b1_col, PS[:, 6, 0:E * HB], SH).then_inc(b1_in_s, 1)
                act.wait_ge(experts_loaded, 48)
                nc.scalar.mul(W1_p[0], W1_in, SW).then_inc(high_in, 1)
                nc.scalar.mul(W2_p[0], W2_in, SW).then_inc(high_in, 1)
                act.wait_ge(var_ready, 1)
                nc.scalar.activation(tmp[:, 2, :], tmp[:, 0, :], ACT.Sqrt).then_inc(root_ready, 1)
                for c in range(PANELS):
                    act.wait_ge(turned_done, c + 1)
                    nc.scalar.mul(xT[0][:, SUB * c:SUB * c + SUB, :].rearrange("p s f -> p (s f)"), PS[:, c % 2, :],
                                  SX).then_inc(xT_high, 1)
                act.wait_ge(w_arg, 1)
                nc.scalar.activation(wts[:, 1, :], wts[:, 0, :], ACT.Exp).then_inc(w_exp, 1)
                for c in range(PANELS):
                    act.wait_ge(combT_done, c + 1)
                    nc.scalar.copy(comb_T[0:E, SUB * c:SUB * c + SUB, :].rearrange("p s f -> p (s f)"),
                                   PS[0:E, c % 2, :]).then_inc(combT_in, 1)

            @block.vector
            def _(dve):
                n = [0]

                def link(ins):
                    n[0] += 1
                    ins.then_inc(chain, 1)
                    dve.wait_ge(chain, n[0])

                def low_part(low, src, scale, high):
                    return nc.vector.scalar_tensor_tensor(low, src, scale, high, ALU.mult, ALU.subtract)

                norm_stats(dve, "g", stats, tmp, root_ready, var_ready)
                dve.wait_ge(high_in, 1)
                low_part(Wg_p[1], Wg_in, SW, Wg_p[0]).then_inc(low_in, 1)
                for c in range(PANELS + 1):
                    if c < PANELS:
                        if c >= 2:
                            dve.wait_ge(turned_done, c - 1)
                        for s in range(SUB):
                            last = normalise(normed[c % 2][:, s, :], SUB * c + s)
                        last.then_inc(normed_ready, 1)
                    if c:
                        dve.wait_ge(xT_high, c)
                        high, low = (xT[k][:, SUB * (c - 1):SUB * c, :].rearrange("p s f -> p (s f)") for k in range(2))
                        low_part(low, PS[:, (c - 1) % 2, :], SX, high).then_inc(xT_low, 1)
                dve.wait_ge(high_in, 4)
                low_part(W1_p[1], W1_in, SW, W1_p[0]).then_inc(low_in, 1)
                low_part(W2_p[1], W2_in, SW, W2_p[0]).then_inc(low_in, 1)
                dve.wait_ge(loaded, 16 * n_loads)
                link(nc.vector.tensor_tensor(gate_b[:, 2, :], gate_b[:, 0, :], gate_b[:, 1, :], ALU.add))
                dve.wait_ge(logits_done, PANELS)
                link(nc.vector.scalar_tensor_tensor(
                    logits, PS[:, 7, 0:TILES * E].rearrange("p (t e) -> p t e", t=TILES), 1.0 / (SX * SW),
                    gate_b[:, 2, :].rearrange("p (o e) -> p o e", o=1).to_broadcast((P, TILES, E)),
                    ALU.mult, ALU.add))
                for t in range(TILES):
                    last = nc.vector.max(top8[:, t, :], logits[:, t, :])
                link(last)
                nc.vector.tensor_tensor(wts[:, 0, :], top8[:, :, 1], top8[:, :, 0], ALU.subtract).then_inc(w_arg, 1)
                for t in range(TILES):
                    last = nc.vector.max_index(idx8[:, t, :], top8[:, t, :], logits[:, t, :])
                link(last)
                link(nc.vector.tensor_copy(idxf, idx8))
                dve.wait_ge(w_exp, 1)
                link(nc.vector.tensor_scalar(wts[:, 0, :], wts[:, 1, :], 1.0, SW * SH, ALU.add, ALU.mult))
                link(nc.vector.reciprocal(wts[:, 2, :], wts[:, 0, :]))
                nc.vector.tensor_tensor(wts[:, 3, :], wts[:, 1, :], wts[:, 2, :], ALU.mult)
                dve.wait_ge(iota_ready, 1)

                def over_experts(v):
                    return v.rearrange("p (t o) -> p t o", o=1).to_broadcast((P, TILES, E))

                iota_all = iota_f.rearrange("p (o e) -> p o e", o=1).to_broadcast((P, TILES, E))
                for k in range(2):
                    last = nc.vector.tensor_tensor(comb_k[:, k], iota_all, over_experts(idxf[:, :, k]), ALU.is_equal)
                link(last)
                for k in range(2):
                    last = nc.vector.tensor_tensor(comb_k[:, k], comb_k[:, k], over_experts(wts[:, 2 + k, :]), ALU.mult)
                link(last)
                nc.vector.tensor_tensor(comb, comb_k[:, 0], comb_k[:, 1], ALU.add).then_inc(comb_ready, 1)
                for c in range(PANELS):
                    dve.wait_ge(bias_done, c + 1)
                    x4 = X[:, SUB * c:SUB * c + SUB, :]
                    nc.vector.tensor_tensor(x4, x4, PS[:, 2 + c % 2, :].rearrange("p (s f) -> p s f", s=SUB), ALU.add)\
                        .then_inc(bias_added, 1)

        def expert_stage():
            L = "e_"
            hid32 = [take([HB, PW]) for _ in range(2)]
            hid = [[take([HB, PW], F16, 2) for _ in range(2)] for _ in range(2)]
            h_done = sem(L + "h_done")
            h_in = sem(L + "h_in")
            h_high_even = sem(L + "h_high_even")
            h_high_odd = sem(L + "h_high_odd")
            h_low_even = sem(L + "h_low_even")
            h_low_odd = sem(L + "h_low_odd")
            y_done = sem(L + "y_done")
            y_used = sem(L + "y_used")
            stored = sem(L + "stored")
            block = ctx2.enter_context(nc.Block())

            @block.sync
            def _(sp):
                xv = X[:].rearrange("p (c s) f -> p c (s f)", s=SUB)
                for c in range(PANELS):
                    sp.wait_ge(y_used, E * (c + 1) + 2)
                    for g in range(GROUPS):
                        sp.dma_start(out_g[g][:, c, :], xv[32 * g:32 * g + 32, c, :]).then_inc(stored, 16)
                sp.wait_ge(stored, 16 * GROUPS * PANELS)

            @block.tensor
            def _(pe):
                pe.sem_inc(y_done, 2)

                def hidden(c, e):
                    for b in range(HB):
                        pe.wait_ge(h_in, c * (E * HB) + HB * e + b + 1)
                        for n, (x_part, w_part) in enumerate(PARTS):
                            last = nc.tensor.matmul(PS[:, (HB * e + b) % 4, :],
                                                    W1_p[w_part][:, e, b * P:b * P + P],
                                                    xT[x_part][:, bass.ds(c * SUB, SUB), :],
                                                    start=(n == 0), stop=(n == len(PARTS) - 1))
                        last.then_inc(h_done, 1)

                def down(c, e):
                    pe.wait_ge(h_low_even, c * E + e + 1)
                    pe.wait_ge(h_low_odd, c * E + e + 1)
                    pe.wait_ge(y_used, c * E + e + 1)
                    for s in range(SUB):
                        for b in range(HB):
                            for n, (h_part, w_part) in enumerate(PARTS):
                                last = nc.tensor.matmul(PS[:, 4 + e % 2, s * F:s * F + F],
                                                        hid[e % 2][h_part][:, b, s * P:s * P + P],
                                                        W2_p[w_part][:, HB * e + b, :],
                                                        start=(b == 0 and n == 0),
                                                        stop=(b == HB - 1 and n == len(PARTS) - 1))
                    last.then_inc(y_done, 1)

                hidden(0, 0)
                with pe.Fori(0, PANELS - 1) as c:
                    for e in range(E):
                        hidden(*((c, e + 1) if e < E - 1 else (c + 1, 0)))
                        down(c, e)
                for e in range(E):
                    if e < E - 1:
                        hidden(PANELS - 1, e + 1)
                    down(PANELS - 1, e)

            @block.scalar
            def _(act):
                act.sem_inc(h_in, 4)
                with act.Fori(0, PANELS) as c:
                    for e in range(E):
                        act.wait_ge(y_done, c * E + e + 1)
                        for b in range(HB):
                            src = PS[:, (HB * e + b) % 4, :]
                            act.wait_ge(h_done, c * (E * HB) + HB * e + b + 1)
                            if b == 0:
                                nc.scalar.activation(hid[e % 2][0][:, b, :], src, ACT.Relu, scale=SH / (SX * SW),
                                                     bias=b1_col[:, HB * e + b:HB * e + b + 1]).then_inc(h_high_even, 1)
                            nc.scalar.activation(hid32[e % 2][:, b, :], src, ACT.Relu, scale=SH / (SX * SW),
                                                 bias=b1_col[:, HB * e + b:HB * e + b + 1]).then_inc(h_in, 1)

            @block.gpsimd
            def _(pool):
                with pool.Fori(0, PANELS) as c:
                    for e in range(E):
                        pool.wait_ge(h_high_even, c * E + e + 1)
                        pool.wait_ge(h_in, c * (E * HB) + HB * e + 4 + 1)
                        nc.gpsimd.tensor_tensor(hid[e % 2][1][:, 0, :], hid32[e % 2][:, 0, :], hid[e % 2][0][:, 0, :],
                                                ALU.subtract).then_inc(h_low_even, 1)

            @block.vector
            def _(dve):
                dve.sem_inc(y_used, 2)

                def odd_parts(c, e):
                    dve.wait_ge(h_in, c * (E * HB) + HB * e + 4 + 2)
                    nc.vector.tensor_copy(hid[e % 2][0][:, 1, :], hid32[e % 2][:, 1, :]).then_inc(h_high_odd, 1)
                    dve.wait_ge(h_high_odd, c * E + e + 1)
                    nc.vector.tensor_tensor(hid[e % 2][1][:, 1, :], hid32[e % 2][:, 1, :], hid[e % 2][0][:, 1, :],
                                            ALU.subtract).then_inc(h_low_odd, 1)

                def add(c, e):
                    dve.wait_ge(y_done, c * E + e + 3)
                    dve.wait_ge(y_used, c * E + e + 2)
                    for s in range(SUB):
                        t = X[:, c * SUB + s, :]
                        last = nc.vector.scalar_tensor_tensor(t, PS[:, 4 + e % 2, s * F:s * F + F],
                                                              comb[:, c * SUB + s, e:e + 1], t, ALU.mult, ALU.add)
                    last.then_inc(y_used, 1)

                odd_parts(0, 0)
                with dve.Fori(0, PANELS - 1) as c:
                    for e in range(E):
                        odd_parts(*((c, e + 1) if e < E - 1 else (c + 1, 0)))
                        add(c, e)
                for e in range(E):
                    if e < E - 1:
                        odd_parts(PANELS - 1, e + 1)
                    add(PANELS - 1, e)

        for stage in (lambda: node_stage(0), lambda: attention_stage(0), lambda: node_stage(1),
                      lambda: attention_stage(1), gate_stage, expert_stage):
            with ExitStack() as ctx2:
                stage()


_INS = ['x', 'adj', 'L0_gnn_W', 'L0_gnn_a', 'L0_ffn_weight', 'L0_ffn_bias', 'L1_gnn_W', 'L1_gnn_a', 'L1_ffn_Wg',
        'L1_ffn_bg', 'L1_ffn_bias', 'L1_ffn_W1', 'L1_ffn_b1', 'L1_ffn_W2', 'L1_ffn_b2']


def kernel(**inputs):
    import numpy as _np
    import concourse.bacc as _bacc
    from concourse import mybir as _mybir
    from concourse.bass_utils import run_bass_kernel_spmd as _run

    nc = _bacc.Bacc("TRN2", target_bir_lowering=False, num_devices=1, dynamic_dma_scratch_size=8192)
    arrays, args = {}, []
    for name in _INS:
        a = _np.ascontiguousarray(inputs[name])
        arrays[f"in_{name}"] = a
        args.append(nc.dram_tensor(f"in_{name}", a.shape, _mybir.dt.from_np(a.dtype), kind="ExternalInput").ap())
    args.append(nc.dram_tensor("out_x", (4096, 128), _mybir.dt.float32, kind="ExternalOutput").ap())
    gnn_moe_kernel(nc, *args)
    r = _run(nc, [arrays], core_ids=[0])
    return r.results[0]["out_x"]
```

```python
from contextlib import ExitStack

import numpy as np

import concourse.bass as bass
from concourse import mybir

F32 = mybir.dt.float32
F16 = mybir.dt.float16
F8 = mybir.dt.float8e4
U8 = mybir.dt.uint8
U16 = mybir.dt.uint16
U32 = mybir.dt.uint32
ALU = mybir.AluOpType
ACT = mybir.ActivationFunctionType
AX = mybir.AxisListType

N = 4096
P = 128
F = 128
TILES = N // P
GROUPS = 4
SUB = 4
PANELS = TILES // SUB
PW = SUB * P
LAST_PANEL = range(TILES - SUB, TILES)
E = 8
HID = 256
HB = HID // P
EPS = 1e-5
ALPHAS = (0.01, 0.2)
ONE_BYTE = 0x38
VCOLS = 2 * (F + 1)
V_SCALE = 256.0
LOW = 2048.0
BIG = 2.0 ** 100
SX, SW, SH, SB = 4.0, 64.0, 16.0, 64.0


def gnn_moe_kernel(nc, x, adj, W0, a0, Wf, bf, W1, a1, Wg, bg, gbias, We1, be1, We2, be2, out):
    x_g = x.rearrange("(g c q s) f -> g q c (s f)", g=GROUPS, c=PANELS, q=32, s=SUB)
    out_g = out.rearrange("(g c q s) f -> g q c (s f)", g=GROUPS, c=PANELS, q=32, s=SUB)
    adj_g = adj.rearrange("(b c q s) (g k) -> c s g q b k", b=GROUPS, c=PANELS, q=32, s=SUB, g=GROUPS)

    with ExitStack() as ctx:
        def sb(name, shape, dt):
            return ctx.enter_context(nc.sbuf_tensor(name, shape, dt))

        def wait_alone(eng, semaphore, value):
            eng.wait_ge(semaphore, value)
            eng.sem_inc(passed[str(eng.engine)], 1)

        def sem(name):
            return ctx.enter_context(nc.semaphore(name))

        passed = {str(e.engine): sem(f"passed_{n}")
                  for n, e in (("pe", nc.tensor), ("act", nc.scalar), ("dve", nc.vector), ("pool", nc.gpsimd))}
        s1_rows = nc.dram_tensor("s1_rows", [2, TILES, P], F32)
        prep_w = nc.dram_tensor("prep_w", [P, 2 * F + 2], F32)

        mask = sb("mask", [P, PANELS, PANELS, PW * SUB], U8)
        X = sb("X", [P, TILES, F], F32)
        V = [sb(f"V{m}", [P, TILES, VCOLS], F16) for m in range(2)]
        val = V[1][:].rearrange("p t c -> p (t c)").bitcast(F32).rearrange("p (t c) -> p t c", t=TILES)[:, :, 0:F]
        s1_row = sb("s1_row", [P, 2, PW], F32)
        ident = sb("ident", [P, P], F32)
        S12 = sb("S12", [P, 2, TILES], F32)
        neg_s2 = sb("neg_s2", [P, TILES], F32)
        s2_big = sb("s2_big", [P, TILES], F32)
        stats = sb("stats", [P, TILES, 6], F32)
        AC = sb("AC", [P, 2, TILES], F32)
        BD = sb("BD", [P, 2, TILES], F32)
        den_high = sb("den_high", [P, 2, TILES], F16)
        den_low = sb("den_low", [P, 2, TILES], F16)
        den_rest = sb("den_rest", [P, 2, TILES], F32)
        smax = sb("smax", [P, 2], F32)
        mean = sb("mean", [P, TILES], F32)
        rstd = sb("rstd", [P, TILES], F32)
        rden = sb("rden", [P, SUB], F32)

        def at(buf, start, shape, dt, size):
            n = int(np.prod(shape))
            flat = buf[:, start:start + n * size].bitcast(dt)
            if len(shape) == 1:
                return flat
            names = "abcd"[:len(shape)]
            return flat.rearrange(f"p ({' '.join(names)}) -> p {' '.join(names)}",
                                  **{k: v for k, v in zip(names, shape)})

        raw = sb("raw", [P, 2, GROUPS, 1024], U8)
        turned = sb("turned", [P, PANELS, P], U32)
        work = sb("work", [P, 20640], U8)
        gate8 = [at(work, 2048 * n, [PW, SUB], U8, 1) for n in range(2)]
        ring = [[at(work, 4096 + 4096 * n + 2048 * m, [PW * SUB], U8, 1) for m in range(2)] for n in range(2)]
        scaled = [at(work, 12288 + 2064 * n, [2, VCOLS], F32, 4) for n in range(2)]
        summed = at(work, 16416, [SUB, VCOLS], F32, 4)
        product = [[at(work, 12288 + 4096 * n + 2048 * m, [SUB, F], F32, 4) for m in range(2)] for n in range(2)]

        def carve(buf):
            o = [0]

            def take(shape, dt=F32, size=4):
                r = at(buf, o[0], shape, dt, size)
                o[0] += int(np.prod(shape)) * size
                return r
            return take

        PS = ctx.enter_context(nc.psum_tensor("PS", [P, 8, 512], F32))

        def acc(ib, m):
            return PS[:, 2 * ib + m, 0:VCOLS]

        take_raw = carve(raw[:].rearrange("p a b c -> p (a b c)"))
        W1_ext = take_raw([F + 2])
        Wf_T = take_raw([F])
        bias_row = take_raw([F])
        VF1 = take_raw([2, TILES])
        next_loaded = sem("next_loaded")

        raw_ready = [sem(f"raw_ready{n}") for n in range(2)]
        raw_used = sem("raw_used")
        mask_ready = sem("mask_ready")

        def load_adj(pool, w, n, groups=range(GROUPS)):
            if not (isinstance(w, int) and 4 * w + n < 2):
                pool.wait_ge(raw_used, 4 * w + n - 1)
            for g in groups:
                pool.dma_start(raw[32 * g:32 * g + 32, n % 2], adj_g[w, n, g], max_dma_last_dim=4096)\
                    .then_inc(raw_ready[n % 2], 16)

        def turn(dve, w, n):
            if not (isinstance(w, int) and 4 * w + n == 0):
                dve.wait_ge(mask_ready, 4 * w + n)
            dve.wait_ge(raw_ready[n % 2], 64 * (2 * w + n // 2 + 1))
            nc.vector.transpose(turned[:].rearrange("p c (b q) -> p b c q", b=GROUPS),
                                raw[:, n % 2].bitcast(U32).rearrange("p b (c q) -> p b c q", q=32))\
                .then_inc(raw_used, 1)

        def settle(act, w, n, panels=range(PANELS)):
            act.wait_ge(raw_used, 4 * w + n + 1)
            part = nc.scalar.mul(mask[:, w, panels.start:panels.stop, 4 * P * n:4 * P * n + 4 * P].bitcast(U16),
                                 turned[:].rearrange("p c i -> p (c i)").bitcast(U16)
                                 .rearrange("p (c i) -> p c i", c=PANELS)[:, panels.start:panels.stop],
                                 float(ONE_BYTE))
            if panels.stop == PANELS:
                part.then_inc(mask_ready, 1)

        rows_loaded = [sem(f"row_loaded{k}") for k in range(2)]
        all_gates = [sem(f"gates{k}") for k in range(2)]
        all_gates_last = [sem(f"gates_last{k}") for k in range(2)]

        def gate(w, j, subs):
            for s in subs:
                last = nc.vector.tensor_scalar(gate8[j % 2][:, :, s], s1_row[:, w % 2, :],
                                               neg_s2[:, SUB * j + s:SUB * j + s + 1], float(ONE_BYTE),
                                               ALU.is_gt, ALU.mult)
            return last

        def act_gate(w, j):
            return nc.scalar.activation(gate8[j % 2][:, :, SUB - 1], s1_row[:, w % 2, :], ACT.Relu, scale=BIG,
                                        bias=s2_big[:, SUB * j + SUB - 1:SUB * j + SUB])

        def row(layer, w):
            return s1_rows[layer, bass.ds(w * SUB, SUB), :].rearrange("(o s) p -> o (s p)", o=1).to_broadcast((P, PW))

        def norm_stats(dve, tag, tmp, root_ready, var_ready):
            chain = sem(tag + "_stats_chain")
            n = [0]

            def link(ins):
                n[0] += 1
                ins.then_inc(chain, 1)
                dve.wait_ge(chain, n[0])

            nc.vector.tensor_tensor(mean[:], stats[:, :, 1], stats[:, :, 4], ALU.add)
            nc.vector.tensor_tensor(tmp[:, 1, :], stats[:, :, 2], stats[:, :, 5], ALU.add)
            link(nc.vector.tensor_tensor(tmp[:, 0, :], stats[:, :, 1], stats[:, :, 4], ALU.subtract))
            nc.vector.tensor_scalar(mean[:], mean[:], 0.5, None, ALU.mult)
            link(nc.vector.tensor_tensor(tmp[:, 0, :], tmp[:, 0, :], tmp[:, 0, :], ALU.mult))
            link(nc.vector.scalar_tensor_tensor(tmp[:, 0, :], tmp[:, 0, :], F / 4.0, tmp[:, 1, :], ALU.mult, ALU.add))
            nc.vector.tensor_scalar(tmp[:, 0, :], tmp[:, 0, :], 1.0 / F, EPS, ALU.mult, ALU.add).then_inc(var_ready, 1)
            dve.wait_ge(root_ready, 1)
            link(nc.vector.reciprocal(rstd[:], tmp[:, 2, :]))
            link(nc.vector.tensor_tensor(tmp[:, 3, :], rstd[:], rstd[:], ALU.mult))
            link(nc.vector.tensor_tensor(tmp[:, 3, :], tmp[:, 3, :], tmp[:, 0, :], ALU.mult))
            link(nc.vector.tensor_scalar(tmp[:, 3, :], tmp[:, 3, :], -0.5, 1.5, ALU.mult, ALU.add))
            link(nc.vector.tensor_tensor(rstd[:], rstd[:], tmp[:, 3, :], ALU.mult))

        def normalise(dst, t):
            return nc.vector.tensor_scalar(dst, X[:, t, :], mean[:, t:t + 1], rstd[:, t:t + 1],
                                           ALU.subtract, ALU.mult)

        def node_stage(layer):
            L = f"n{layer}_"
            take = carve(work)
            x_T = [take([PW]) for _ in range(2)]
            tmp = [take([4, TILES]) for _ in range(1 + layer)]
            warg = take([3, TILES])
            s1_T = take([P])
            neg_mr = take([TILES])
            spare = take([2])
            W_in = take([2, F])
            a_cols = take([2, 2])
            W_T = take([3, F])
            W_sum = take([2, 3])
            W_c = take([3, F])
            W_back = take([2, F + 2])
            Wf_back = take([F])
            W_ext = (W_back[:, 0, :], W1_ext)[layer]
            VF = VF1
            alpha = ALPHAS[layer]

            if layer == 0:
                x_loaded = [sem(f"{L}x_loaded{h}") for h in range(2)]
                loaded = sem(L + "loaded")
                ident_ready = sem(L + "ident_ready")
                weights_T = sem(L + "weights_T")
                weights_in = sem(L + "weights_in")
                summed_w = sem(L + "summed_w")
                centred = sem(L + "centred")
                centred_T = sem(L + "centred_T")
                prepared = sem(L + "prepared")
                kept = sem(L + "kept")
                mr_ready = sem(L + "mr_ready")
                val_in_act = sem(L + "val_in_act")
            var_ready = [sem(f"{L}var_ready{k}") for k in range(1 + layer)]
            root_ready = [sem(f"{L}root_ready{k}") for k in range(1 + layer)]
            turned_done = sem(L + "turned_done")
            turned_in = sem(L + "turned_in")
            prod_done = sem(L + "prod_done")
            x_added = sem(L + "x_added")
            s12_in = sem(L + "s12_in")
            val_in = sem(L + "val_in")
            stats_read = sem(L + "stats_read")
            bias_in = sem(L + "bias_in") if layer else None
            s12_scaled = sem(L + "s12_scaled")
            pmax = sem(L + "pmax")
            allmax = sem(L + "allmax")
            warg0 = sem(L + "warg0")
            args_ready = sem(L + "args_ready")
            exps_ready = sem(L + "exps_ready")
            factors_ready = sem(L + "factors_ready") if layer else None
            neg_ready = sem(L + "neg_ready")
            s1T_done = sem(L + "s1T_done")
            s1T_in = sem(L + "s1T_in")
            row0_done = sem(L + "row0_done")
            rows_out = sem(L + "rows_out")

            ahead = 3
            chunks = [(k, c - k * ahead) for c in range(PANELS + layer * ahead) for k in range(1 + layer)
                      if 0 <= c - k * ahead < PANELS]
            step = {kc: q for q, kc in enumerate(chunks)}
            block = ctx2.enter_context(nc.Block())

            def bank_T(q):
                return PS[:, q % 2, :]

            def products(q):
                b = 2 + 2 * (q % 2)
                return PS[:, b:b + 2, :].rearrange("p b (h f) -> p (b h) f", h=2)

            def tiles(c):
                return X[:, SUB * c:SUB * c + SUB, :]

            @block.sync
            def _(sp):
                if layer == 0:
                    half = PANELS // 2

                    def load_x(h):
                        for g in range(GROUPS):
                            xv = X[32 * g:32 * g + 32].rearrange("p (c s) f -> p c (s f)", s=SUB)
                            sp.dma_start(xv[:, half * h:half * h + half], x_g[g][:, half * h:half * h + half])\
                                .then_inc(x_loaded[h], 16)

                    load_x(0)
                    sp.dma_start(W_in[:, 0, :], W0).then_inc(loaded, 16)
                    sp.dma_start(W_in[:, 1, :], W1).then_inc(loaded, 16)
                    sp.dma_start(W_T[:, 2, :], Wf).then_inc(loaded, 16)
                    for k, a in enumerate((a0, a1)):
                        with nc.allow_non_contiguous_dma(reason="256 scalars"):
                            sp.dma_start(a_cols[:, k, :], a.rearrange("(c p) one -> p (c one)", c=2))\
                                .then_inc(loaded, 16)
                    load_x(1)
                    sp.wait_ge(prepared, 1)
                    sp.dma_start(prep_w[:, 0:F + 2], W_back[:, 1, :]).then_inc(kept, 16)
                    sp.dma_start(prep_w[:, F + 2:2 * F + 2], Wf_back).then_inc(kept, 16)
                    sp.wait_ge(kept, 32)
                sp.wait_ge(s1T_in, 1)
                sp.dma_start(s1_rows[layer], s1_T[0:TILES, :]).then_inc(rows_out, 16)
                sp.wait_ge(rows_out, 16)
                sp.wait_ge(rows_loaded[layer], 16)
                sp.dma_start(s1_row[:, 1, :], row(layer, 1)).then_inc(rows_loaded[layer], 16)

            @block.gpsimd
            def _(pool):
                if layer == 0:
                    nc.gpsimd.memset(ident[:], 0.0).then_inc(ident_ready, 1)
                    pool.wait_ge(ident_ready, 1)
                    nc.gpsimd.affine_select(out=ident[:], in_=ident[:], compare_op=ALU.not_equal, fill=1.0,
                                            base=0, pattern=[[-1, P]], channel_multiplier=1).then_inc(ident_ready, 1)
                    for h in range(2):
                        pool.wait_ge(x_loaded[h], 16 * GROUPS)
                        load_adj(pool, 0, h)
                    load_adj(pool, 0, 2)
                    load_adj(pool, 0, 3)
                    load_adj(pool, 1, 0)
                    load_adj(pool, 1, 1)
                else:
                    for c in range(PANELS):
                        pool.wait_ge(turned_done, step[0, c] + 1)
                        if c == PANELS - 1:
                            pool.wait_ge(stats_read, 1)
                        nc.gpsimd.tensor_tensor(tiles(c), tiles(c), bias_row.rearrange("p (o f) -> p o f", o=1)
                                                .to_broadcast((P, SUB, F)), ALU.add).then_inc(bias_in, 1)
                pool.wait_ge(pmax, 1)
                nc.gpsimd.partition_all_reduce(smax[:, 1:2], smax[:, 0:1], P, bass.bass_isa.ReduceOp.max)\
                    .then_inc(allmax, 1)

            @block.tensor
            def _(pe):
                if layer == 0:
                    pe.wait_ge(ident_ready, 2)
                    pe.wait_ge(loaded, 16 * 5)
                    nc.tensor.transpose(PS[:, 6, 0:P], W_in[:, 0, :], ident[:])
                    nc.tensor.transpose(PS[:, 6, P:2 * P], W_in[:, 1, :], ident[:]).then_inc(weights_T, 1)
                    pe.wait_ge(centred, 1)
                    for k in range(3):
                        last = nc.tensor.transpose(PS[:, 7, k * P:k * P + P], W_c[:, k, :], ident[:])
                    for k in range(2):
                        last = nc.tensor.matmul(PS[:, 6, 2 * k:2 * k + 2], W_c[:, k, :], a_cols[:, k, :],
                                                start=True, stop=True)
                    last.then_inc(centred_T, 1)

                def to_T(q):
                    k, c = chunks[q]
                    if layer == 0 and c % (PANELS // 2) == 0:
                        pe.wait_ge(x_loaded[c // (PANELS // 2)], 16 * GROUPS)
                    if k:
                        pe.wait_ge(x_added, c + 1)
                    if q >= 2:
                        pe.wait_ge(turned_in, q - 1)
                    for s in range(SUB):
                        last = nc.tensor.transpose(bank_T(q)[:, s * P:s * P + P], X[:, SUB * c + s, :], ident[:])
                    last.then_inc(turned_done, 1)

                to_T(0)
                if layer == 0:
                    pe.wait_ge(prepared, 1)
                for q, (k, c) in enumerate(chunks):
                    if q + 1 < len(chunks):
                        to_T(q + 1)
                    pe.wait_ge(turned_in, q + 1)
                    if q >= 2:
                        k2, c2 = chunks[q - 2]
                        if k2 == layer:
                            pe.wait_ge(s12_in, c2 + 1)
                        pe.wait_ge(val_in if k2 else x_added, c2 + 1)
                    rhs = Wf_T if k < layer else W_ext
                    for s in range(SUB):
                        last = nc.tensor.matmul(products(q)[:, s, 0:rhs.shape[1]], x_T[q % 2][:, s * P:s * P + P],
                                                rhs, start=True, stop=True)
                    last.then_inc(prod_done, 1)
                pe.wait_ge(s12_scaled, 1)
                nc.tensor.transpose(PS[0:TILES, 6, 0:P], S12[:, 0, :], ident[:]).then_inc(s1T_done, 1)
                for s in range(SUB):
                    last = nc.tensor.matmul(PS[:, 7, s * P:s * P + P], S12[:, 0, s:s + 1].to_broadcast((P, P)),
                                            ident[:], start=True, stop=True)
                last.then_inc(row0_done, 1)

            def outs(act, q):
                c = chunks[q][1]
                act.wait_ge(prod_done, q + 1)
                nc.scalar.copy(S12[:, :, SUB * c:SUB * c + SUB].rearrange("p k s -> p s k"),
                               products(q)[:, :, F:F + 2]).then_inc(s12_in, 1)
                if layer == 1:
                    nc.scalar.copy(val[:, SUB * c:SUB * c + SUB, :], products(q)[:, :, 0:F]).then_inc(val_in, 1)

            def root(act, k):
                act.wait_ge(var_ready[k], 1)
                nc.scalar.activation(tmp[k][:, 2, :], tmp[k][:, 0, :], ACT.Sqrt).then_inc(root_ready[k], 1)
                if k == layer:
                    nc.scalar.activation(spare[:, 1:2], ident[:, 0:1], ACT.Exp)

            def normalise_half(act, c):
                for s in (2, 3):
                    t = SUB * c + s
                    last = nc.scalar.activation(val[:, t, :], X[:, t, :], ACT.Identity, scale=rstd[:, t:t + 1],
                                                bias=neg_mr[:, t:t + 1])
                last.then_inc(val_in_act, 1)

            @block.scalar
            def _(act):
                if layer == 0:
                    act.wait_ge(weights_T, 1)
                    nc.scalar.copy(W_T[:, 0:2, :].rearrange("p k f -> p (k f)"), PS[:, 6, 0:2 * P])\
                        .then_inc(weights_in, 1)
                    act.wait_ge(centred_T, 1)
                    nc.scalar.copy(W_back[:, :, 0:F], PS[:, 7, 0:2 * P].rearrange("p (k f) -> p k f", k=2))
                    nc.scalar.copy(Wf_back, PS[:, 7, 2 * P:3 * P])
                    nc.scalar.copy(W_back[:, :, F:F + 2], PS[:, 6, 0:4].rearrange("p (k f) -> p k f", k=2))\
                        .then_inc(prepared, 1)
                if layer == 1:
                    nc.scalar.activation(spare[:, 0:1], ident[:, 0:1], ACT.Sqrt)
                for q, (k, c) in enumerate(chunks):
                    if layer == 1 and q == 1:
                        root(act, 0)
                    act.wait_ge(turned_done, q + 1)
                    if q >= 2:
                        act.wait_ge(prod_done, q - 1)
                    nc.scalar.copy(x_T[q % 2], bank_T(q)).then_inc(turned_in, 1)
                    if layer == 1 and q == len(chunks) - 1:
                        root(act, 1)
                    if q and chunks[q - 1][0] == layer:
                        outs(act, q - 1)
                    if layer == 0 and c == 1:
                        root(act, 0)
                        act.wait_ge(mr_ready, 1)
                        normalise_half(act, 0)
                    if layer == 0 and c:
                        normalise_half(act, c)
                    if layer == 0 and c in (2, 4, 6):
                        settle(act, 0, c // 2 - 1)
                outs(act, len(chunks) - 1)
                if layer == 0:
                    settle(act, 0, 3)
                act.wait_ge(s1T_done, 1)
                nc.scalar.copy(s1_T[0:TILES, :], PS[0:TILES, 6, 0:P]).then_inc(s1T_in, 1)
                act.wait_ge(row0_done, 1)
                nc.scalar.copy(s1_row[:, 0, :], PS[:, 7, :]).then_inc(rows_loaded[layer], 16)
                act.wait_ge(args_ready, 1)
                nc.scalar.activation(BD[:, 0, :], warg[:, 2, :], ACT.Exp).then_inc(exps_ready, 1)
                nc.scalar.activation(BD[:, 1, :], warg[:, 2, :], ACT.Exp, scale=alpha).then_inc(exps_ready, 1)
                nc.scalar.activation(AC[:], warg[:, 0:2, :], ACT.Exp).then_inc(exps_ready, 1)
                act.wait_ge(neg_ready, 1)
                act.wait_ge(rows_loaded[layer], 16)
                act_gate(0, 0).then_inc(all_gates_last[layer], 1)

            @block.vector
            def _(dve):
                def add(c):
                    q = step[0, c]
                    dve.wait_ge(prod_done, q + 1)
                    if layer == 1:
                        dve.wait_ge(bias_in, c + 1)
                    else:
                        dve.wait_ge(s12_in, c + 1)
                        dve.wait_ge(val_in, c + 1)
                        dve.wait_ge(val_in_act, c + 1)
                    for s in range(SUB):
                        t = SUB * c + s
                        last = nc.vector.scalar_tensor_tensor(X[:, t, :], products(q)[:, s, 0:F], rstd[:, t:t + 1],
                                                              X[:, t, :], ALU.mult, ALU.add)
                    last.then_inc(x_added, 1)

                def statistics(tiles):
                    for t in tiles:
                        last = nc.vector.bn_stats(stats[:, t, :], X[:, t, :])
                    return last

                if layer == 0:
                    dve.wait_ge(x_loaded[0], 16 * GROUPS)
                    statistics(range(TILES // 2))
                    dve.wait_ge(loaded, 16 * 5)
                    dve.wait_ge(weights_in, 1)
                    nc.vector.tensor_reduce(W_sum[:, 0, :], W_T, AX.X, ALU.add).then_inc(summed_w, 1)
                    dve.wait_ge(summed_w, 1)
                    nc.vector.tensor_scalar(W_sum[:, 1, :], W_sum[:, 0, :], 1.0 / F, None, ALU.mult)\
                        .then_inc(summed_w, 1)
                    dve.wait_ge(summed_w, 2)
                    nc.vector.tensor_tensor(W_c, W_T, W_sum[:, 1, :].rearrange("p (k o) -> p k o", o=1)
                                            .to_broadcast((P, 3, F)), ALU.subtract).then_inc(centred, 1)
                    dve.wait_ge(x_loaded[1], 16 * GROUPS)
                    last = statistics(range(TILES // 2, TILES))
                else:
                    last = statistics(LAST_PANEL)
                last.then_inc(stats_read, 1)
                dve.wait_ge(stats_read, 1)
                norm_stats(dve, f"{L}0", tmp[0], root_ready[0], var_ready[0])
                if layer == 0:
                    nc.vector.scalar_tensor_tensor(neg_mr, mean[:], -1.0, rstd[:], ALU.mult, ALU.mult)\
                        .then_inc(mr_ready, 1)
                for c in range(PANELS):
                    if layer == 0:
                        for s in (0, 1):
                            last = normalise(val[:, SUB * c + s, :], SUB * c + s)
                        last.then_inc(val_in, 1)
                    add(c)
                    if layer == 0 and c % 2 == 0:
                        turn(dve, 0, c // 2)
                    if layer == 1:
                        dve.wait_ge(x_added, c + 1)
                        last = statistics(range(SUB * c, SUB * c + SUB))
                if layer == 1:
                    last.then_inc(stats_read, 1)
                    dve.wait_ge(stats_read, 2)
                    norm_stats(dve, f"{L}1", tmp[1], root_ready[1], var_ready[1])
                dve.wait_ge(s12_in, PANELS)
                nc.vector.tensor_tensor(S12[:], S12[:], rstd[:].rearrange("p (o t) -> p o t", o=1)
                                        .to_broadcast((P, 2, TILES)), ALU.mult).then_inc(s12_scaled, 1)
                dve.wait_ge(s12_scaled, 1)
                nc.vector.tensor_reduce(smax[:, 0:1], S12[:, 1, :], AX.X, ALU.max).then_inc(pmax, 1)
                nc.vector.tensor_scalar(neg_s2[:], S12[:, 1, :], -1.0, None, ALU.mult)
                nc.vector.tensor_scalar(s2_big[:], S12[:, 1, :], BIG, None, ALU.mult).then_inc(neg_ready, 1)
                dve.wait_ge(neg_ready, 1)
                dve.wait_ge(allmax, 1)
                nc.vector.tensor_scalar(warg[:, 2, :], S12[:, 1, :], smax[:, 1:2], None, ALU.subtract)
                nc.vector.tensor_scalar(warg[:, 0, :], S12[:, 0, :], smax[:, 1:2], 1.0 - alpha,
                                        ALU.add, ALU.mult).then_inc(warg0, 1)
                dve.wait_ge(warg0, 1)
                nc.vector.tensor_scalar(warg[:, 1, :], warg[:, 0, :], -1.0, 0.0, ALU.mult, ALU.min).then_inc(warg0, 1)
                dve.wait_ge(warg0, 2)
                nc.vector.tensor_scalar(warg[:, 0, :], warg[:, 0, :], 0.0, None, ALU.min).then_inc(args_ready, 1)
                dve.wait_ge(rows_loaded[layer], 16)
                gate(0, 0, (0, 1, 2)).then_inc(all_gates[layer], 1)
                dve.wait_ge(exps_ready, 2)
                if layer == 1:
                    nc.vector.scalar_tensor_tensor(VF, BD[:], V_SCALE, rstd[:].rearrange("p (o t) -> p o t", o=1)
                                                   .to_broadcast((P, 2, TILES)), ALU.mult, ALU.mult)\
                        .then_inc(factors_ready, 1)
                    dve.wait_ge(factors_ready, 1)
                nc.vector.tensor_scalar(BD[:], BD[:], V_SCALE, None, ALU.mult)

        def attention_stage(layer):
            L = f"a{layer}_"
            row_loaded = rows_loaded[layer]
            den_high_in = sem(L + "den_high_in")
            den_rest_ready = sem(L + "den_rest_ready")
            den_low_in = sem(L + "den_low_in")
            den_cols = sem(L + "den_cols")
            product_ready = sem(L + "product_ready")
            v_high = sem(L + "v_high")
            v_rest = sem(L + "v_rest")
            v_low = sem(L + "v_low")
            den_in = sem(L + "den_in")
            gates, gates_last = all_gates[layer], all_gates_last[layer]
            m1_ready = sem(L + "m1_ready")
            masks_ready = sem(L + "masks_ready")
            masks_used = sem(L + "masks_used")
            acc_done = sem(L + "acc_done")
            acc_out = sem(L + "acc_out")
            scaled_used = sem(L + "scaled_used")
            lows_scaled = sem(L + "lows_scaled")
            summed_ready = sem(L + "summed_ready")
            rden_ready = sem(L + "rden_ready")
            summed_used = sem(L + "summed_used")
            last_chain = sem(L + "last_chain")
            block = ctx2.enter_context(nc.Block())

            @block.sync
            def _(sp):
                with sp.Fori(2, PANELS) as w:
                    sp.wait_ge(row_loaded, 16 * w)
                    sp.wait_ge(gates, PANELS * (w - 1))
                    sp.wait_ge(gates_last, PANELS * (w - 1))
                    sp.dma_start(s1_row[:, w % 2, :], row(layer, w)).then_inc(row_loaded, 16)
                if layer == 0:
                    sp.wait_ge(raw_used, TILES)
                    sp.dma_start(W1_ext, prep_w[:, 0:F + 2]).then_inc(next_loaded, 16)
                    sp.dma_start(Wf_T, prep_w[:, F + 2:2 * F + 2]).then_inc(next_loaded, 16)
                    sp.dma_start(bias_row, bf.rearrange("(o f) -> o f", o=1).to_broadcast((P, F)))\
                        .then_inc(next_loaded, 16)
                    sp.wait_ge(next_loaded, 48)
                if layer == 1:
                    sp.dma_start(W1_in, We1.rearrange("e d h -> d e h")).then_inc(experts_loaded, 16)
                    for h in range(2):
                        sp.dma_start(W2_in.rearrange("p (e b) f -> p e b f", e=E)[:, 4 * h:4 * h + 4],
                                     We2.rearrange("e (b p) f -> p e b f", b=HB)[:, 4 * h:4 * h + 4])\
                            .then_inc(experts_loaded, 16)

            def finish(dve, w):
                dve.wait_ge(summed_ready, w + 1)
                dve.wait_ge(summed_used, w + 1)
                nc.vector.reciprocal(rden[:], summed[:, :, F]).then_inc(rden_ready, 1)
                dve.wait_ge(rden_ready, w + 1)
                for ib in range(SUB):
                    t = X[:, w * SUB + ib, :]
                    last = nc.vector.scalar_tensor_tensor(t, summed[:, ib, 0:F], rden[:, ib:ib + 1], t,
                                                          ALU.mult, ALU.add)
                last.then_inc(summed_used, 1)

            def finish_last(dve):
                w = PANELS - 1
                n = [0]

                def link(ins):
                    n[0] += 1
                    ins.then_inc(last_chain, 1)
                    dve.wait_ge(last_chain, n[0])

                dve.wait_ge(summed_used, w + 1)
                for ib in range(SUB):
                    dve.wait_ge(acc_out, 4 * w + 4 + ib + 1)
                    nc.vector.tensor_tensor(summed[:, ib, :], scaled[ib % 2][:, 0, :], scaled[ib % 2][:, 1, :],
                                            ALU.add).then_inc(scaled_used, 1)
                    dve.wait_ge(scaled_used, 4 * w + 2 + ib + 1)
                    link(nc.vector.scalar_tensor_tensor(summed[:, ib, 0:F + 1], summed[:, ib, F + 1:VCOLS], 1.0 / LOW,
                                                        summed[:, ib, 0:F + 1], ALU.mult, ALU.add))
                    link(nc.vector.reciprocal(rden[:, ib:ib + 1], summed[:, ib, F:F + 1]))
                    t = X[:, w * SUB + ib, :]
                    nc.vector.scalar_tensor_tensor(t, summed[:, ib, 0:F], rden[:, ib:ib + 1], t, ALU.mult, ALU.add)

            def products(dve, c):
                for m in range(2):
                    if c >= 2:
                        dve.wait_ge(v_low, 2 * c - 3 + m)
                    factor = (BD, VF1)[layer][:, m, SUB * c:SUB * c + SUB].rearrange("p (s o) -> p s o", o=1)\
                        .to_broadcast((P, SUB, F))
                    nc.vector.tensor_tensor(product[c % 2][m], val[:, SUB * c:SUB * c + SUB, :], factor, ALU.mult)\
                        .then_inc(product_ready, 1)

            def norm_panel(w):
                for ib in range(SUB):
                    t = w * SUB + ib
                    nc.vector.bn_stats(stats[:, bass.ds(t, 1), :].rearrange("p o c -> p (o c)"),
                                       X[:, bass.ds(t, 1), :].rearrange("p o c -> p (o c)"))

            def gate_last(act, w, j, first):
                if not (first and j < 2):
                    wait_alone(act, m1_ready, PANELS * w + j - 1)
                act_gate(w, j).then_inc(gates_last, 1)

            def panel(dve, w, first, final):
                for j in range(PANELS):
                    if layer == 0 and j == 0:
                        dve.wait_ge(mask_ready, 4 * w + 4)
                    dve.wait_ge(gates, PANELS * w + j + 1)
                    dve.wait_ge(gates_last, PANELS * w + j + 1)
                    dve.wait_ge(masks_used, PANELS * w + j + 1)
                    m1, m2 = (r.bitcast(U32) for r in ring[j % 2])
                    adj_w = mask[:, w, j, :].bitcast(U32)
                    nc.vector.tensor_tensor(m1, adj_w, gate8[j % 2].rearrange("p i s -> p (i s)").bitcast(U32),
                                            ALU.bitwise_and).then_inc(m1_ready, 1)
                    if first and j == 0:
                        dve.wait_ge(m1_ready, 1)
                        nc.vector.tensor_tensor(m2, adj_w, m1, ALU.bitwise_xor).then_inc(masks_ready, 1)
                    if first and j + 1 < PANELS:
                        products(dve, j + 1)
                    more = not (final and j == PANELS - 1)
                    nw, nj = (w, j + 1) if j < PANELS - 1 else (w + 1, 0)
                    if more:
                        if nj == 0:
                            dve.wait_ge(row_loaded, 16 * nw + 16)
                        if not (first and j == 0):
                            dve.wait_ge(m1_ready, PANELS * w + j)
                        gate(nw, nj, (0, 1))
                    if not (first and j == 0):
                        dve.wait_ge(m1_ready, PANELS * w + j + 1)
                        nc.vector.tensor_tensor(m2, adj_w, m1, ALU.bitwise_xor).then_inc(masks_ready, 1)
                    if layer == 0 and not final and j % 2 == 0:
                        turn(dve, w + 1, j // 2)
                    if more:
                        gate(nw, nj, (2,)).then_inc(gates, 1)
                    if not first and j == 3:
                        finish(dve, w - 1)
                    if not first and j == 5:
                        wait_alone(dve, summed_used, w + 1)
                        norm_panel(w - 1)

            @block.vector
            def _(dve):
                dve.sem_inc(summed_used, 1)
                products(dve, 0)
                dve.wait_ge(den_high_in, 1)
                nc.vector.tensor_tensor(den_rest[:], BD[:], den_high[:], ALU.subtract).then_inc(den_rest_ready, 1)
                panel(dve, 0, True, False)
                with dve.Fori(1, PANELS - 1) as w:
                    panel(dve, w, False, False)
                panel(dve, PANELS - 1, False, True)
                finish_last(dve)

            @block.tensor
            def _(pe):
                pe.sem_inc(masks_used, 2)
                pe.wait_ge(den_cols, 1)
                with pe.Fori(0, PANELS) as w:
                    for j in range(PANELS):
                        pe.wait_ge(v_low, 2 * j + 2)
                        pe.wait_ge(den_in, j + 1)
                        wait_alone(pe, masks_ready, PANELS * w + j + 1)
                        for ib in range(SUB):
                            if j == 0:
                                wait_alone(pe, acc_out, 4 * w + ib + 1)
                            for s in range(SUB):
                                for m in range(2):
                                    lhs = ring[j % 2][m].bitcast(F8).rearrange("p (i s) -> p s i", s=SUB)
                                    last = nc.tensor.matmul(acc(ib, m), lhs[:, s, ib * P:ib * P + P],
                                                            V[m][:, SUB * j + s, :],
                                                            start=(j == 0 and s == 0),
                                                            stop=(j == PANELS - 1 and s == SUB - 1))
                            if j == PANELS - 1 and ib < SUB - 1:
                                last.then_inc(acc_done, 1)
                        last.then_inc(masks_used, 1)

            def drain_sums(act, w, tiles):
                for ib in tiles:
                    if ib < SUB - 1:
                        act.wait_ge(acc_done, (SUB - 1) * w + ib + 1)
                    else:
                        act.wait_ge(masks_used, PANELS * w + PANELS + 2)
                    act.wait_ge(scaled_used, 4 * w + ib + 1)
                    for m in range(2):
                        last = nc.scalar.activation(scaled[ib % 2][:, m, :], acc(ib, m), ACT.Identity,
                                                    scale=AC[:, m, bass.ds(w * SUB + ib, 1)])
                    last.then_inc(acc_out, 1)

            def end_panel(act, w, more):
                if more:
                    act.wait_ge(row_loaded, 16 * w + 32)
                    gate_last(act, w + 1, 0, False)
                    if layer == 0 and not (isinstance(w, int) and w == 0):
                        settle(act, w + 1, 3)
                    gate_last(act, w + 1, 1, False)
                drain_sums(act, w, (0,))
                if more:
                    gate_last(act, w + 1, 2, False)
                drain_sums(act, w, (1, 2, 3))
                if more:
                    gate_last(act, w + 1, 3, False)

            def high_parts(act, c):
                for m in range(2):
                    act.wait_ge(product_ready, 2 * c + 1 + m)
                    nc.scalar.copy(V[m][:, SUB * c:SUB * c + SUB, 0:F], product[c % 2][m]).then_inc(v_high, 1)

            @block.scalar
            def _(act):
                act.sem_inc(acc_out, 4)
                nc.scalar.copy(den_high[:], BD[:]).then_inc(den_high_in, 1)
                high_parts(act, 0)
                act.wait_ge(den_rest_ready, 1)
                nc.scalar.mul(den_low[:], den_rest[:], LOW).then_inc(den_low_in, 1)
                act.wait_ge(den_low_in, 1)
                nc.scalar.copy(V[0][:, :, F], den_high[:, 0, :])
                nc.scalar.copy(V[0][:, :, 2 * F + 1], den_low[:, 0, :]).then_inc(den_cols, 1)
                gate_last(act, 0, 1, True)
                for c in range(PANELS):
                    if 0 < c < PANELS - 1:
                        high_parts(act, c + 1)
                    for m in range(2):
                        act.wait_ge(v_rest, 2 * c + 1 + m)
                        nc.scalar.mul(V[m][:, SUB * c:SUB * c + SUB, F + 1:2 * F + 1], product[c % 2][m], LOW)\
                            .then_inc(v_low, 1)
                    if c == 0:
                        high_parts(act, 1)
                    if c + 2 < PANELS:
                        gate_last(act, 0, c + 2, True)
                    if layer == 0:
                        half = PANELS // 2
                        settle(act, 1, c // 2, range(half * (c % 2), half * (c % 2) + half))
                act.wait_ge(v_low, 2 * PANELS)
                end_panel(act, 0, True)
                with act.Fori(1, PANELS - 1) as w:
                    if layer == 0:
                        settle(act, w + 1, 0)
                    gate_last(act, w, 4, False)
                    if layer == 0:
                        settle(act, w + 1, 1)
                    gate_last(act, w, 5, False)
                    gate_last(act, w, 6, False)
                    if layer == 0:
                        settle(act, w + 1, 2)
                    gate_last(act, w, 7, False)
                    end_panel(act, w, True)
                for j in range(SUB, PANELS):
                    gate_last(act, PANELS - 1, j, False)
                    if layer == 1 and j < SUB + 2:
                        k = j - SUB
                        whole, parts = ((W1_in, W1_p), (W2_in, W2_p))[k]
                        act.wait_ge(experts_loaded, 48)
                        nc.scalar.mul(whole, whole, SW).then_inc(experts_scaled, 1)
                        act.wait_ge(experts_scaled, k + 1)
                        nc.scalar.copy(parts[0], whole).then_inc(experts_high, 1)
                end_panel(act, PANELS - 1, False)

            @block.gpsimd
            def _(pool):
                pool.sem_inc(scaled_used, 2)

                def den_columns(c):
                    pool.wait_ge(product_ready, 2 * c + 2)
                    nc.gpsimd.tensor_copy(V[1][:, SUB * c:SUB * c + SUB, F], den_high[:, 1, SUB * c:SUB * c + SUB])
                    nc.gpsimd.tensor_copy(V[1][:, SUB * c:SUB * c + SUB, 2 * F + 1],
                                          den_low[:, 1, SUB * c:SUB * c + SUB]).then_inc(den_in, 1)

                def add(w):
                    for ib in range(SUB):
                        pool.wait_ge(acc_out, 4 * w + 4 + ib + 1)
                        if ib == 0:
                            pool.wait_ge(summed_used, w + 1)
                        nc.gpsimd.tensor_tensor(summed[:, ib, :], scaled[ib % 2][:, 0, :], scaled[ib % 2][:, 1, :],
                                                ALU.add).then_inc(scaled_used, 1)
                    wait_alone(pool, scaled_used, 4 * w + 6)
                    lows = summed[:, :, F + 1:VCOLS]
                    nc.gpsimd.tensor_scalar(lows, lows, 1.0 / LOW, 0.0, ALU.mult, ALU.add).then_inc(lows_scaled, 1)
                    pool.wait_ge(lows_scaled, w + 1)
                    nc.gpsimd.tensor_tensor(summed[:, :, 0:F + 1], summed[:, :, 0:F + 1], lows, ALU.add)\
                        .then_inc(summed_ready, 1)

                for c in range(PANELS):
                    for m in range(2):
                        pool.wait_ge(v_high, 2 * c + m + 1)
                        nc.gpsimd.tensor_tensor(product[c % 2][m], product[c % 2][m],
                                                V[m][:, SUB * c:SUB * c + SUB, 0:F], ALU.subtract).then_inc(v_rest, 1)
                    if c == 0:
                        pool.wait_ge(den_cols, 1)
                    den_columns(c)
                    if layer == 0 and c:
                        for k in (c - 1, c)[:2 if c == PANELS - 1 else 1]:
                            n = 2 + k // 2
                            load_adj(pool, 1 + n // 4, n % 4, range(2 * (k % 2), 2 * (k % 2) + 2))
                pool.wait_ge(v_low, 2 * PANELS)
                if layer == 0:
                    add(0)
                    with pool.Fori(1, PANELS - 2) as w:
                        load_adj(pool, w + 1, 2)
                        load_adj(pool, w + 1, 3)
                        load_adj(pool, w + 2, 0)
                        load_adj(pool, w + 2, 1)
                        add(w)
                    load_adj(pool, PANELS - 1, 2)
                    load_adj(pool, PANELS - 1, 3)
                    add(PANELS - 2)
                else:
                    with pool.Fori(0, PANELS - 1) as w:
                        add(w)
                    for k, (whole, parts) in enumerate(((W1_in, W1_p), (W2_in, W2_p))):
                        pool.wait_ge(experts_high, k + 1)
                        nc.gpsimd.tensor_tensor(parts[1], whole, parts[0], ALU.subtract).then_inc(experts_low, 1)
                    pool.wait_ge(experts_low, 2)

        take = carve(mask[:].rearrange("p a b c -> p (a b c)"))
        PARTS = ((0, 0), (0, 1), (1, 0))
        W1_in = take([E, HID])
        W2_in = take([E * HB, F])
        W1_p = [take([E, HID], F16, 2) for _ in range(2)]
        W2_p = [take([E * HB, F], F16, 2) for _ in range(2)]
        xT = [take([TILES, P], F16, 2) for _ in range(2)]
        b1_col = take([E * HB])
        comb = take([TILES, E])
        experts_loaded = sem("experts_loaded")
        experts_scaled = sem("experts_scaled")
        experts_high = sem("experts_high")
        experts_low = sem("experts_low")

        def moe_stage():
            L = "m_"
            Wg_in = take([E])
            Wg_p = [take([E], F16, 2) for _ in range(2)]
            gate_b = take([3, E])
            b1_in = take([P])
            b2_blocks = take([SUB * F])
            normed = [take([SUB, F]) for _ in range(4)]
            logits = take([TILES, E])
            top8 = take([TILES, 8])
            idx8 = take([TILES, 8], U32)
            idxf = take([TILES, 8])
            iota_f = take([E])
            wts = take([4, TILES])
            comb_k = take([2, TILES, E])
            b2_p = [take([SUB * F], F16, 2) for _ in range(2)]
            comb_T = [take([2, P], F16, 2) for _ in range(2)]
            spare = take([2])
            neg_mr = take([TILES])
            tmp = take([4, TILES])
            loaded = sem(L + "loaded")
            b2_zero = sem(L + "b2_zero")
            b2_loaded = sem(L + "b2_loaded")
            b2_high = sem(L + "b2_high")
            b2_low = sem(L + "b2_low")
            b1_done = sem(L + "b1_done")
            high_in = sem(L + "high_in")
            low_in = sem(L + "low_in")
            b1_scaled = sem(L + "b1_scaled")
            iota_ready = sem(L + "iota_ready")
            chain = sem(L + "chain")
            var_ready = sem(L + "var_ready")
            root_ready = sem(L + "root_ready")
            mr_ready = sem(L + "mr_ready")
            normed_ready = sem(L + "normed_ready")
            normed_act = sem(L + "normed_act")
            turned_done = sem(L + "turned_done")
            xT_high = sem(L + "xT_high")
            xT_low = sem(L + "xT_low")
            logits_done = sem(L + "logits_done")
            w_arg = sem(L + "w_arg")
            w_exp = sem(L + "w_exp")
            comb_ready = sem(L + "comb_ready")
            combT_done = sem(L + "combT_done")
            combT_high = sem(L + "combT_high")
            combT_low = sem(L + "combT_low")
            bias_done = sem(L + "bias_done")
            bias_added = sem(L + "bias_added")
            n_loads = 4
            hid32 = [take([HB, PW]) for _ in range(2)]
            hid = [[take([HB, PW], F16, 2) for _ in range(2)] for _ in range(2)]
            h_done = sem(L + "h_done")
            h_in = sem(L + "h_in")
            h_high_even = sem(L + "h_high_even")
            h_high_odd = sem(L + "h_high_odd")
            h_low_even = sem(L + "h_low_even")
            h_low_odd = sem(L + "h_low_odd")
            y_done = sem(L + "y_done")
            y_used = sem(L + "y_used")
            stored = sem(L + "stored")
            block = ctx2.enter_context(nc.Block())

            @block.sync
            def _(sp):
                sp.dma_start(Wg_in, Wg).then_inc(loaded, 16)
                for k, b in enumerate((bg, gbias)):
                    sp.dma_start(gate_b[:, k, :], b.rearrange("(o e) -> o e", o=1).to_broadcast((P, E)))\
                        .then_inc(loaded, 16)
                sp.dma_start(b1_in[0:E * HB, :], be1.rearrange("e (b p) -> (e b) p", b=HB)).then_inc(loaded, 16)
                sp.wait_ge(b2_zero, 1)
                for k in range(4):
                    for s in range(SUB):
                        sp.dma_start(b2_blocks[32 * k + E * s:32 * k + E * s + E, s * F:s * F + F], be2)\
                            .then_inc(b2_loaded, 16)

                xv = X[:].rearrange("p (c s) f -> p c (s f)", s=SUB)
                for c in range(PANELS):
                    if c == 0:
                        sp.wait_ge(bias_added, PANELS)
                    sp.wait_ge(y_used, E * (c + 1) + 2)
                    for g in range(GROUPS):
                        sp.dma_start(out_g[g][:, c, :], xv[32 * g:32 * g + 32, c, :]).then_inc(stored, 16)
                sp.wait_ge(stored, 16 * GROUPS * PANELS)

            @block.gpsimd
            def _(pool):
                nc.gpsimd.memset(b2_blocks, 0.0).then_inc(b2_zero, 1)
                nc.gpsimd.iota(iota_f, pattern=[[1, E]], base=0, channel_multiplier=0,
                               allow_small_or_imprecise_dtypes=True).then_inc(iota_ready, 1)

                with pool.Fori(0, PANELS) as c:
                    for e in range(E):
                        pool.wait_ge(h_high_even, c * E + e + 1)
                        pool.wait_ge(h_in, c * (E * HB) + HB * e + 4 + 1)
                        nc.gpsimd.tensor_tensor(hid[e % 2][1][:, 0, :], hid32[e % 2][:, 0, :], hid[e % 2][0][:, 0, :],
                                                ALU.subtract).then_inc(h_low_even, 1)

            @block.tensor
            def _(pe):
                pe.sem_inc(y_done, 2)
                pe.wait_ge(loaded, 16 * n_loads)
                nc.tensor.transpose(PS[:, 6, 0:E * HB], b1_in[0:E * HB, :], ident[0:E * HB, 0:E * HB])\
                    .then_inc(b1_done, 1)

                def gate_logits(c):
                    pe.wait_ge(xT_low, c + 1)
                    for s in range(SUB):
                        t = SUB * c + s
                        for n, (x_part, w_part) in enumerate(PARTS):
                            last = nc.tensor.matmul(PS[:, 7, t * E:t * E + E], xT[x_part][:, t, :], Wg_p[w_part],
                                                    start=(n == 0), stop=(n == len(PARTS) - 1))
                    last.then_inc(logits_done, 1)

                for c in range(PANELS):
                    pe.wait_ge(normed_ready, c + 1)
                    pe.wait_ge(normed_act, c + 1)
                    if c >= 4:
                        pe.wait_ge(xT_low, c - 3)
                    for s in range(SUB):
                        last = nc.tensor.transpose(PS[:, c % 4, s * P:s * P + P], normed[c % 4][:, s, :], ident[:])
                    last.then_inc(turned_done, 1)
                    if c == 1:
                        pe.wait_ge(low_in, 1)
                    if c >= 2:
                        gate_logits(c - 2)
                gate_logits(PANELS - 2)
                gate_logits(PANELS - 1)

                def hidden(c, e):
                    for b in range(HB):
                        pe.wait_ge(h_in, c * (E * HB) + HB * e + b + 1)
                        for n, (x_part, w_part) in enumerate(PARTS):
                            last = nc.tensor.matmul(PS[:, (HB * e + b) % 4, :],
                                                    W1_p[w_part][:, e, b * P:b * P + P],
                                                    xT[x_part][:, bass.ds(c * SUB, SUB), :],
                                                    start=(n == 0), stop=(n == len(PARTS) - 1))
                        last.then_inc(h_done, 1)

                def down(c, e):
                    pe.wait_ge(h_low_even, c * E + e + 1)
                    pe.wait_ge(h_low_odd, c * E + e + 1)
                    pe.wait_ge(y_used, c * E + e + 1)
                    for s in range(SUB):
                        for b in range(HB):
                            for n, (h_part, w_part) in enumerate(PARTS):
                                last = nc.tensor.matmul(PS[:, 4 + e % 2, s * F:s * F + F],
                                                        hid[e % 2][h_part][:, b, s * P:s * P + P],
                                                        W2_p[w_part][:, HB * e + b, :],
                                                        start=(b == 0 and n == 0),
                                                        stop=(b == HB - 1 and n == len(PARTS) - 1))
                    last.then_inc(y_done, 1)

                def bias(c):
                    if c >= 2:
                        pe.wait_ge(bias_added, c - 1)
                    rows = slice(SUB * E * (c % 4), SUB * E * (c % 4) + SUB * E)
                    for n, (c_part, b_part) in enumerate(PARTS):
                        last = nc.tensor.matmul(PS[:, 6 + c % 2, :], comb_T[c_part][rows, c // 4, :],
                                                b2_p[b_part][rows, :], start=(n == 0), stop=(n == len(PARTS) - 1))
                    last.then_inc(bias_done, 1)

                hidden(0, 0)
                for e in range(E):
                    hidden(*((0, e + 1) if e < E - 1 else (1, 0)))
                    down(0, e)
                    if e == E - 2:
                        pe.wait_ge(comb_ready, 1)
                        for h in range(2):
                            nc.tensor.transpose(PS[:, 6 + h, 0:P], comb[:, TILES // 2 * h:TILES // 2 * (h + 1), :]
                                                .rearrange("p t e -> p (t e)"), ident[:]).then_inc(combT_done, 1)
                for e in range(E):
                    hidden(*((1, e + 1) if e < E - 1 else (2, 0)))
                    down(1, e)
                    if e == 0:
                        pe.wait_ge(b2_low, 1)
                        pe.wait_ge(combT_low, 2)
                    bias(e)
                with pe.Fori(2, PANELS - 1) as c:
                    for e in range(E):
                        hidden(*((c, e + 1) if e < E - 1 else (c + 1, 0)))
                        down(c, e)
                for e in range(E):
                    if e < E - 1:
                        hidden(PANELS - 1, e + 1)
                    down(PANELS - 1, e)

            @block.scalar
            def _(act):
                act.sem_inc(h_in, 4)
                nc.scalar.activation(spare[:, 0:1], ident[:, 0:1], ACT.Sqrt)
                act.wait_ge(var_ready, 1)
                nc.scalar.activation(tmp[:, 2, :], tmp[:, 0, :], ACT.Sqrt).then_inc(root_ready, 1)
                nc.scalar.activation(spare[:, 1:2], ident[:, 0:1], ACT.Exp)
                act.wait_ge(mr_ready, 1)

                def normalise_half(c):
                    if c >= 4:
                        act.wait_ge(turned_done, c - 3)
                    for s in (2, 3):
                        t = SUB * c + s
                        last = nc.scalar.activation(normed[c % 4][:, s, :], X[:, t, :], ACT.Identity,
                                                    scale=rstd[:, t:t + 1], bias=neg_mr[:, t:t + 1])
                    last.then_inc(normed_act, 1)

                normalise_half(0)
                normalise_half(1)
                act.wait_ge(loaded, 16 * n_loads)
                nc.scalar.mul(Wg_p[0], Wg_in, SW).then_inc(high_in, 1)
                act.wait_ge(b1_done, 1)
                nc.scalar.mul(b1_col, PS[:, 6, 0:E * HB], SH).then_inc(b1_scaled, 1)
                for c in range(PANELS):
                    if c + 2 < PANELS:
                        normalise_half(c + 2)
                    act.wait_ge(turned_done, c + 1)
                    nc.scalar.mul(xT[0][:, SUB * c:SUB * c + SUB, :].rearrange("p s f -> p (s f)"), PS[:, c % 4, :],
                                  SX).then_inc(xT_high, 1)

                def high_part(e, b, src):
                    return nc.scalar.activation(hid[e % 2][0][:, b, :], src, ACT.Relu, scale=SH / (SX * SW),
                                                bias=b1_col[:, HB * e + b:HB * e + b + 1])

                def hidden_parts(c, e):
                    act.wait_ge(y_done, c * E + e + 1)
                    for b in range(HB):
                        src = PS[:, (HB * e + b) % 4, :]
                        act.wait_ge(h_done, c * (E * HB) + HB * e + b + 1)
                        if b == 0:
                            high_part(e, b, src).then_inc(h_high_even, 1)
                        elif isinstance(c, int):
                            high_part(e, b, src).then_inc(h_high_odd, 1)
                        nc.scalar.activation(hid32[e % 2][:, b, :], src, ACT.Relu, scale=SH / (SX * SW),
                                             bias=b1_col[:, HB * e + b:HB * e + b + 1]).then_inc(h_in, 1)

                def exp_of(a, b, n):
                    act.wait_ge(w_arg, n)
                    nc.scalar.activation(wts[:, 1, a:b], wts[:, 0, a:b], ACT.Exp).then_inc(w_exp, 1)

                hidden_parts(0, 0)
                exp_of(0, SUB, 1)
                for e in range(1, E):
                    hidden_parts(0, e)
                    if e == 3:
                        exp_of(SUB, TILES, 2)
                    elif e == 4:
                        act.wait_ge(b2_loaded, 16 * 4 * SUB)
                        nc.scalar.mul(b2_p[0], b2_blocks, SB).then_inc(b2_high, 1)
                for h in range(2):
                    act.wait_ge(combT_done, h + 1)
                    nc.scalar.mul(comb_T[0][:, h, :], PS[:, 6 + h, 0:P], SW * SH).then_inc(combT_high, 1)
                with act.Fori(1, PANELS) as c:
                    for e in range(E):
                        hidden_parts(c, e)

            @block.vector
            def _(dve):
                dve.sem_inc(y_used, 2)
                n = [0]

                def link(ins):
                    n[0] += 1
                    ins.then_inc(chain, 1)
                    dve.wait_ge(chain, n[0])

                def low_part(low, src, scale, high):
                    return nc.vector.scalar_tensor_tensor(low, src, scale, high, ALU.mult, ALU.subtract)

                def odd_parts(c, e):
                    dve.wait_ge(h_in, c * (E * HB) + HB * e + 4 + 2)
                    if not (isinstance(c, int) and c == 0):
                        nc.vector.tensor_copy(hid[e % 2][0][:, 1, :], hid32[e % 2][:, 1, :]).then_inc(h_high_odd, 1)
                    dve.wait_ge(h_high_odd, c * E + e + 1)
                    nc.vector.tensor_tensor(hid[e % 2][1][:, 1, :], hid32[e % 2][:, 1, :], hid[e % 2][0][:, 1, :],
                                            ALU.subtract).then_inc(h_low_odd, 1)

                def add(c, e):
                    dve.wait_ge(y_done, c * E + e + 3)
                    dve.wait_ge(y_used, c * E + e + 2)
                    for s in range(SUB):
                        t = X[:, c * SUB + s, :]
                        last = nc.vector.scalar_tensor_tensor(t, PS[:, 4 + e % 2, s * F:s * F + F],
                                                              comb[:, c * SUB + s, e:e + 1], t, ALU.mult, ALU.add)
                    last.then_inc(y_used, 1)

                for t in LAST_PANEL:
                    last = nc.vector.bn_stats(stats[:, t, :], X[:, t, :])
                link(last)
                norm_stats(dve, "g", tmp, root_ready, var_ready)
                link(nc.vector.tensor_tensor(neg_mr, mean[:], rstd[:], ALU.mult))
                nc.vector.tensor_scalar(neg_mr, neg_mr, -1.0, None, ALU.mult).then_inc(mr_ready, 1)
                for c in range(PANELS + 2):
                    if c < PANELS:
                        if c >= 4:
                            dve.wait_ge(turned_done, c - 3)
                        for s in (0, 1):
                            last = normalise(normed[c % 4][:, s, :], SUB * c + s)
                        last.then_inc(normed_ready, 1)
                    if c == 1:
                        dve.wait_ge(high_in, 1)
                        low_part(Wg_p[1], Wg_in, SW, Wg_p[0]).then_inc(low_in, 1)
                    if c >= 2:
                        d = c - 2
                        dve.wait_ge(xT_high, d + 1)
                        high, low = (xT[k][:, SUB * d:SUB * d + SUB, :].rearrange("p s f -> p (s f)") for k in range(2))
                        low_part(low, PS[:, d % 4, :], SX, high).then_inc(xT_low, 1)
                dve.wait_ge(loaded, 16 * n_loads)
                link(nc.vector.tensor_tensor(gate_b[:, 2, :], gate_b[:, 0, :], gate_b[:, 1, :], ALU.add))
                dve.wait_ge(logits_done, PANELS)
                link(nc.vector.scalar_tensor_tensor(
                    logits, PS[:, 7, 0:TILES * E].rearrange("p (t e) -> p t e", t=TILES), 1.0 / (SX * SW),
                    gate_b[:, 2, :].rearrange("p (o e) -> p o e", o=1).to_broadcast((P, TILES, E)),
                    ALU.mult, ALU.add))

                def top_values(a, b):
                    for t in range(a, b):
                        last = nc.vector.max(top8[:, t, :], logits[:, t, :])
                    return last

                def top_places(a, b):
                    for t in range(a, b):
                        last = nc.vector.max_index(idx8[:, t, :], top8[:, t, :], logits[:, t, :])
                    return last

                def differences(a, b):
                    nc.vector.tensor_tensor(wts[:, 0, a:b], top8[:, a:b, 1], top8[:, a:b, 0], ALU.subtract)\
                        .then_inc(w_arg, 1)

                def weigh(a, b):
                    shape = (P, b - a, E)

                    def over_experts(v):
                        return v.rearrange("p (t o) -> p t o", o=1).to_broadcast(shape)

                    link(nc.vector.tensor_copy(idxf[:, a:b], idx8[:, a:b]))
                    link(nc.vector.tensor_scalar(wts[:, 0, a:b], wts[:, 1, a:b], 1.0, SW * SH, ALU.add, ALU.mult))
                    link(nc.vector.reciprocal(wts[:, 2, a:b], wts[:, 0, a:b]))
                    nc.vector.tensor_tensor(wts[:, 3, a:b], wts[:, 1, a:b], wts[:, 2, a:b], ALU.mult)
                    iota_all = iota_f.rearrange("p (o e) -> p o e", o=1).to_broadcast(shape)
                    for k in range(2):
                        last = nc.vector.tensor_tensor(comb_k[:, k, a:b], iota_all, over_experts(idxf[:, a:b, k]),
                                                       ALU.is_equal)
                    link(last)
                    for k in range(2):
                        last = nc.vector.tensor_tensor(comb_k[:, k, a:b], comb_k[:, k, a:b],
                                                       over_experts(wts[:, 2 + k, a:b]), ALU.mult)
                    link(last)
                    return nc.vector.tensor_tensor(comb[:, a:b], comb_k[:, 0, a:b], comb_k[:, 1, a:b], ALU.add)

                link(top_values(0, SUB))
                differences(0, SUB)
                odd_parts(0, 0)
                link(top_places(0, SUB))
                dve.wait_ge(iota_ready, 1)
                dve.wait_ge(w_exp, 1)
                link(weigh(0, SUB))
                for e in range(E):
                    odd_parts(*((0, e + 1) if e < E - 1 else (1, 0)))
                    add(0, e)
                    if e == 0:
                        link(top_values(SUB, TILES))
                        differences(SUB, TILES)
                    elif e in (1, 2, 3):
                        third = -(-(TILES - SUB) // 3)
                        last = top_places(SUB + third * (e - 1), min(SUB + third * e, TILES))
                        if e == 3:
                            link(last)
                    elif e == 4:
                        dve.wait_ge(w_exp, 2)
                        weigh(SUB, TILES).then_inc(comb_ready, 1)
                    elif e == 5:
                        dve.wait_ge(b2_high, 1)
                        low_part(b2_p[1], b2_blocks, SB, b2_p[0]).then_inc(b2_low, 1)
                    elif e == 7:
                        for h in range(2):
                            dve.wait_ge(combT_high, h + 1)
                            low_part(comb_T[1][:, h, :], PS[:, 6 + h, 0:P], SW * SH, comb_T[0][:, h, :])\
                                .then_inc(combT_low, 1)
                dve.wait_ge(comb_ready, 1)
                for e in range(E):
                    odd_parts(*((1, e + 1) if e < E - 1 else (2, 0)))
                    add(1, e)
                    dve.wait_ge(y_used, E + e + 3)
                    dve.wait_ge(bias_done, e + 1)
                    x4 = X[:, SUB * e:SUB * e + SUB, :]
                    nc.vector.scalar_tensor_tensor(x4, PS[:, 6 + e % 2, :].rearrange("p (s f) -> p s f", s=SUB),
                                                   1.0 / SB, x4, ALU.mult, ALU.add).then_inc(bias_added, 1)
                    dve.wait_ge(bias_added, e + 1)
                with dve.Fori(2, PANELS - 1) as c:
                    for e in range(E):
                        odd_parts(*((c, e + 1) if e < E - 1 else (c + 1, 0)))
                        add(c, e)
                for e in range(E):
                    if e < E - 1:
                        odd_parts(PANELS - 1, e + 1)
                    add(PANELS - 1, e)

        for stage in (lambda: node_stage(0), lambda: attention_stage(0), lambda: node_stage(1),
                      lambda: attention_stage(1), moe_stage):
            with ExitStack() as ctx2:
                stage()


_INS = ['x', 'adj', 'L0_gnn_W', 'L0_gnn_a', 'L0_ffn_weight', 'L0_ffn_bias', 'L1_gnn_W', 'L1_gnn_a', 'L1_ffn_Wg',
        'L1_ffn_bg', 'L1_ffn_bias', 'L1_ffn_W1', 'L1_ffn_b1', 'L1_ffn_W2', 'L1_ffn_b2']


def kernel(**inputs):
    import numpy as _np
    import concourse.bacc as _bacc
    from concourse import mybir as _mybir
    from concourse.bass_utils import run_bass_kernel_spmd as _run

    nc = _bacc.Bacc("TRN2", target_bir_lowering=False, num_devices=1, dynamic_dma_scratch_size=8192)
    arrays, args = {}, []
    for name in _INS:
        a = _np.ascontiguousarray(inputs[name])
        arrays[f"in_{name}"] = a
        args.append(nc.dram_tensor(f"in_{name}", a.shape, _mybir.dt.from_np(a.dtype), kind="ExternalInput").ap())
    args.append(nc.dram_tensor("out_x", (4096, 128), _mybir.dt.float32, kind="ExternalOutput").ap())
    gnn_moe_kernel(nc, *args)
    r = _run(nc, [arrays], core_ids=[0])
    return r.results[0]["out_x"]
```
